# Optimizing a Trainium2 kernel written in Bass

```python
import numpy as np
import jax
import jax.numpy as jnp

def _softmax(x, axis=-1):
    return jax.nn.softmax(x, axis=axis)

def _gelu(x):
    return jax.nn.gelu(x, approximate=True)

def _silu(x):
    return jax.nn.silu(x)

def _sigmoid(x):
    return jax.nn.sigmoid(x)

def _layernorm(x, axis=-1, eps=1e-05):
    m = jnp.mean(x, axis=axis, keepdims=True)
    v = jnp.var(x, axis=axis, keepdims=True)
    return (x - m) / jnp.sqrt(v + eps)

def _scatter_add(tgt, idx, src, axis=0):
    return tgt.at[idx].add(src)

def _segment_sum(src, seg, n):
    return jax.ops.segment_sum(src, seg, n)
kernel_name = 'mk_early_fusion_embed_d1_tok_img1024_r4_9fd216'

def setup_inputs(seed: int=0):
    np.random.seed(seed)
    _w = jnp.asarray

    def _rec_inputs():
        import jax
        import jax.numpy as jnp
        _rk = jax.random.key(seed)
        x = -7.10856e-05 + 0.999911 * jax.random.normal(jax.random.fold_in(_rk, 1), (2, 1, 1024, 256), jnp.float32)
        x_txt = jax.random.randint(jax.random.fold_in(_rk, 51), (2, 32), 0, 31993, jnp.int32)
        return (x, x_txt)
    x, x_txt = _rec_inputs()

    def _L0_tok_setup():
        import jax, jax.numpy as jnp
        import numpy as np
        B, T, X, D, H = (16, 1, 1024, 256, 128)
        key = jax.random.key(seed)
        k0, k1, k2 = jax.random.split(key, 3)
        s1 = 1.0 / np.sqrt(D)
        s2 = 1.0 / np.sqrt(H)
        return {'encoder_outputs': jax.random.normal(k0, (B, T, X, D), dtype=jnp.float32), 'W1': jax.random.uniform(k1, (D, H), minval=-s1, maxval=s1, dtype=jnp.float32), 'b1': jnp.zeros((H,), dtype=jnp.float32), 'W2': jax.random.uniform(k2, (H, 1), minval=-s2, maxval=s2, dtype=jnp.float32), 'b2': jnp.zeros((1,), dtype=jnp.float32)}
    _L0_tok_all = _L0_tok_setup()
    _L0_tok_in = {k: v for k, v in _L0_tok_all.items() if k in ('W1', 'b1', 'W2', 'b2')}
    del _L0_tok_all

    def _L0_txt_setup():
        import jax, jax.numpy as jnp
        import numpy as np
        VOCAB = 8000
        key = jax.random.key(seed)
        kx, kw = jax.random.split(key)
        x = jax.random.randint(kx, (4, 512), 0, VOCAB)
        w = jax.random.normal(kw, (VOCAB, 256), dtype=jnp.float32)
        return {'x': x, 'w': w}
    _L0_txt_all = _L0_txt_setup()
    _L0_txt_in = {k: v for k, v in _L0_txt_all.items() if k in ('w',)}
    del _L0_txt_all

    def _L0_attn_setup():
        import jax, jax.numpy as jnp
        import numpy as np
        import math
        H = 16
        EPS = 1e-06

        def _apply_kernel(x, orf):
            m, d_k = orf.shape
            proj = jnp.einsum('bhld,md->bhlm', x, orf) / d_k ** 0.25
            norm = jnp.sum(x * x, axis=-1, keepdims=True) / (2.0 * math.sqrt(d_k))
            return (jnp.exp(proj - norm) + EPS) / math.sqrt(m)
        key = jax.random.key(seed)
        ks = jax.random.split(key, 10)
        B, L, D, m = (4, 1024, 256, 64)
        d_k = D // H
        s = 1.0 / math.sqrt(D)
        return {'x': jax.random.normal(ks[0], (B, L, D), jnp.float32), 'Wq': jax.random.normal(ks[1], (D, D), jnp.float32) * s, 'bq': jax.random.normal(ks[2], (D,), jnp.float32) * s, 'Wk': jax.random.normal(ks[3], (D, D), jnp.float32) * s, 'bk': jax.random.normal(ks[4], (D,), jnp.float32) * s, 'Wv': jax.random.normal(ks[5], (D, D), jnp.float32) * s, 'bv': jax.random.normal(ks[6], (D,), jnp.float32) * s, 'Wo': jax.random.normal(ks[7], (D, D), jnp.float32) * s, 'bo': jax.random.normal(ks[8], (D,), jnp.float32) * s, 'orf': jax.random.normal(ks[9], (m, d_k), jnp.float32)}
    _L0_attn_all = _L0_attn_setup()
    _L0_attn_in = {k: v for k, v in _L0_attn_all.items() if k in ('Wq', 'bq', 'Wk', 'bk', 'Wv', 'bv', 'Wo', 'bo', 'orf')}
    del _L0_attn_all

    def _L0_ffn_setup():
        import jax, jax.numpy as jnp
        import numpy as np
        D_MODEL, D_FF, RANK = (256, 1024, 64)
        B, S = (4, 1024)
        key = jax.random.key(seed)
        ks = jax.random.split(key, 7)
        return {'x': jax.random.normal(ks[0], (B, S, D_MODEL), dtype=jnp.float32), 'U1': jax.random.normal(ks[1], (D_MODEL, RANK), dtype=jnp.float32) * 0.02, 'V1': jax.random.normal(ks[2], (RANK, D_FF), dtype=jnp.float32) * 0.02, 'b1': jnp.zeros((D_FF,), dtype=jnp.float32), 'U2': jax.random.normal(ks[3], (D_FF, RANK), dtype=jnp.float32) * 0.02, 'V2': jax.random.normal(ks[4], (RANK, D_MODEL), dtype=jnp.float32) * 0.02, 'b2': jnp.zeros((D_MODEL,), dtype=jnp.float32)}
    _L0_ffn_all = _L0_ffn_setup()
    _L0_ffn_in = {k: v for k, v in _L0_ffn_all.items() if k in ('U1', 'V1', 'b1', 'U2', 'V2', 'b2')}
    del _L0_ffn_all
    return {'x': x, 'x_txt': x_txt, 'L0_tok_W1': _L0_tok_in['W1'], 'L0_tok_b1': _L0_tok_in['b1'], 'L0_tok_W2': _L0_tok_in['W2'], 'L0_tok_b2': _L0_tok_in['b2'], 'L0_txt_w': _L0_txt_in['w'], 'L0_attn_Wq': _L0_attn_in['Wq'], 'L0_attn_bq': _L0_attn_in['bq'], 'L0_attn_Wk': _L0_attn_in['Wk'], 'L0_attn_bk': _L0_attn_in['bk'], 'L0_attn_Wv': _L0_attn_in['Wv'], 'L0_attn_bv': _L0_attn_in['bv'], 'L0_attn_Wo': _L0_attn_in['Wo'], 'L0_attn_bo': _L0_attn_in['bo'], 'L0_attn_orf': _L0_attn_in['orf'], 'L0_ffn_U1': _L0_ffn_in['U1'], 'L0_ffn_V1': _L0_ffn_in['V1'], 'L0_ffn_b1': _L0_ffn_in['b1'], 'L0_ffn_U2': _L0_ffn_in['U2'], 'L0_ffn_V2': _L0_ffn_in['V2'], 'L0_ffn_b2': _L0_ffn_in['b2']}

def reference(x, x_txt, L0_tok_W1, L0_tok_b1, L0_tok_W2, L0_tok_b2, L0_txt_w, L0_attn_Wq, L0_attn_bq, L0_attn_Wk, L0_attn_bk, L0_attn_Wv, L0_attn_bv, L0_attn_Wo, L0_attn_bo, L0_attn_orf, L0_ffn_U1, L0_ffn_V1, L0_ffn_b1, L0_ffn_U2, L0_ffn_V2, L0_ffn_b2):
    import jax
    import jax.numpy as jnp

    def _L0_tok_ref(encoder_outputs, W1, b1, W2, b2):
        import jax, jax.numpy as jnp
        import numpy as np
        B, T, X, D, H = (16, 1, 1024, 256, 128)
        h = jnp.tanh(encoder_outputs @ W1 + b1)
        energy = h @ W2 + b2
        energy = jnp.transpose(energy, (0, 3, 2, 1))
        weights = jax.nn.softmax(jnp.squeeze(energy, -1), axis=1)
        out = (encoder_outputs * weights[..., None]).sum(axis=1)
        return out

    def _L0_txt_ref(x, w):
        import jax, jax.numpy as jnp
        import numpy as np
        VOCAB = 8000
        one_hot = jax.nn.one_hot(x, w.shape[0], dtype=w.dtype)
        return one_hot @ w

    def _L0_attn_ref(x, Wq, bq, Wk, bk, Wv, bv, Wo, bo, orf):
        import jax, jax.numpy as jnp
        import numpy as np
        import math
        H = 16
        EPS = 1e-06

        def _apply_kernel(x, orf):
            m, d_k = orf.shape
            proj = jnp.einsum('bhld,md->bhlm', x, orf) / d_k ** 0.25
            norm = jnp.sum(x * x, axis=-1, keepdims=True) / (2.0 * math.sqrt(d_k))
            return (jnp.exp(proj - norm) + EPS) / math.sqrt(m)
        B, L, D = x.shape
        d_k = D // H

        def split(y):
            return y.reshape(B, L, H, d_k).transpose(0, 2, 1, 3)
        q = split(x @ Wq.T + bq)
        k = split(x @ Wk.T + bk)
        v = split(x @ Wv.T + bv)
        q_phi = _apply_kernel(q, orf)
        k_phi = _apply_kernel(k, orf)
        kv = jnp.einsum('bhlm,bhld->bhmd', k_phi, v)
        ksum = jnp.sum(k_phi, axis=2)
        num = jnp.einsum('bhlm,bhmd->bhld', q_phi, kv)
        den = jnp.einsum('bhlm,bhm->bhl', q_phi, ksum)
        out = num / den[..., None]
        out = out.transpose(0, 2, 1, 3).reshape(B, L, D)
        return out @ Wo.T + bo

    def _L0_ffn_ref(x, U1, V1, b1, U2, V2, b2):
        import jax, jax.numpy as jnp
        import numpy as np
        D_MODEL, D_FF, RANK = (256, 1024, 64)
        B, S = (4, 1024)
        P = jnp.einsum('bsd,dr->bsr', x, U1)
        H = jax.nn.gelu(jnp.einsum('bsr,rf->bsf', P, V1) + b1)
        Q = jnp.einsum('bsf,fr->bsr', H, U2)
        return jnp.einsum('bsr,rd->bsd', Q, V2) + b2
    h = _L0_tok_ref(x, L0_tok_W1, L0_tok_b1, L0_tok_W2, L0_tok_b2)
    h = jnp.concatenate([h, _L0_txt_ref(x_txt, L0_txt_w)], axis=1)
    h = h + _L0_attn_ref(_layernorm(h, axis=-1), L0_attn_Wq, L0_attn_bq, L0_attn_Wk, L0_attn_bk, L0_attn_Wv, L0_attn_bv, L0_attn_Wo, L0_attn_bo, L0_attn_orf)
    h = h + _L0_ffn_ref(_layernorm(h, axis=-1), L0_ffn_U1, L0_ffn_V1, L0_ffn_b1, L0_ffn_U2, L0_ffn_V2, L0_ffn_b2)
    return h

_drawn_inputs = setup_inputs


def setup_inputs(seed=0):
    import zlib

    import numpy as np

    out = dict(_drawn_inputs(seed))
    spreads = {'L0_tok_b1': (0.0, 0.1), 'L0_ffn_b1': (0.0, 0.8), 'L0_ffn_b2': (0.0, 0.8)}
    factors = {'L0_attn_bq': 8.0,
     'L0_attn_bk': 8.0,
     'L0_ffn_U1': 8.0,
     'L0_ffn_V1': 8.0,
     'L0_ffn_U2': 8.0,
     'L0_ffn_V2': 8.0}
    for name, (base, spread) in spreads.items():
        noise = np.random.default_rng([zlib.crc32(name.encode()), seed]).standard_normal(out[name].shape)
        drawn = base * np.exp(spread * noise) if base else spread * noise
        out[name] = jnp.asarray(drawn.astype(out[name].dtype))
    for name, factor in factors.items():
        out[name] = (out[name] * factor).astype(out[name].dtype)
    return out
```

```python
from contextlib import ExitStack

import concourse.bass as bass
from concourse import mybir

ALU = mybir.AluOpType
ACT = mybir.ActivationFunctionType
AX = mybir.AxisListType
F32 = mybir.dt.float32
I32 = mybir.dt.int32
U32 = mybir.dt.uint32

P = 128
CHUNKS = 3
TILES = 3
KERNEL_EPS = 1e-6
NORM_EPS = 1e-5


def build(nc, x, x_txt, W1, b1t, W2, b2t, emb, WqT, bq, WkT, bk, WvT, bv, WoT, bo, orfT,
          U1, V1, b1f, U2, V2, b2f, ident, norm_block, norm_cols, head_mask, out):
    B, _, X, D = x.shape
    TXT = x_txt.shape[0]
    VOCAB = emb.shape[0]
    L = X + TXT
    N = L // CHUNKS
    ROWS = [P, P, N - 2 * P]
    TXT0 = ROWS[2] - TXT
    KD = D // P
    HID = W1.shape[1]
    DK, M = orfT.shape
    HPH = P // DK
    PAIRS = D // DK // 2
    PPH = PAIRS // KD
    RANK, FF = V1.shape
    FT = FF // P
    RING = 3
    assert KD * P == D and HID == P and 2 * M == P and PPH * 2 * DK == P and N <= 512

    ctx = ExitStack()
    with ctx:
        def sb(name, shape, dt=F32):
            return ctx.enter_context(nc.sbuf_tensor(name, shape, dt))

        def sem(name):
            return ctx.enter_context(nc.semaphore(name))

        w1 = sb("w1", [P, KD, HID])
        b1c = sb("b1c", [P, 1])
        w2 = sb("w2", [P, 1])
        b2c = sb("b2c", [P, 1])
        wq = sb("wq", [P, KD, D])
        wk = sb("wk", [P, KD, D])
        wv = sb("wv", [P, KD, D])
        wo = sb("wo", [P, KD, D])
        bqc = sb("bqc", [P, KD])
        bkc = sb("bkc", [P, KD])
        bvr = sb("bvr", [P, D])
        bor = sb("bor", [P, D])
        orf = sb("orf", [P, HPH * M])
        u1 = sb("u1", [P, KD, RANK])
        v1 = sb("v1", [RANK, FF])
        b1r = sb("b1r", [P, FT])
        u2 = sb("u2", [P, FT, RANK])
        v2 = sb("v2", [RANK, D])
        b2r = sb("b2r", [P, D])
        idn = sb("idn", [P, P])
        nblk = sb("nblk", [P, HPH * M])
        ncol = sb("ncol", [P, HPH])
        mask = sb("mask", [P, P])
        ones = sb("ones", [P, 2 * DK])
        epsm = sb("epsm", [P, P])
        mhalf = sb("mhalf", [P, TILES])
        neps = sb("neps", [P, TILES])
        ids = sb("ids", [TXT, B], I32)
        idf = sb("idf", [TXT, B])
        idc = sb("idc", [TXT, B])
        idu = sb("idu", [TXT, B], U32)
        idok = sb("idok", [TXT, B])
        idle = sb("idle", [TXT, B])
        txt = sb("txt", [TXT, B, D])
        xh = sb("xh", [P, CHUNKS * TILES, D])
        xT = sb("xT", [P, 2, KD, N])
        hT = sb("hT", [P, 2, TILES * P])
        lg = sb("lg", [P, 6, CHUNKS * TILES])
        h = sb("h", [P, CHUNKS * TILES, D])
        hb = sb("hb", [P, CHUNKS * TILES, D])
        st = sb("st", [P, CHUNKS * TILES, 6])
        mv = sb("mv", [P, CHUNKS * TILES, 2])
        ve = sb("ve", [P, CHUNKS * TILES])
        rs = sb("rs", [P, CHUNKS * TILES])
        xln = sb("xln", [P, CHUNKS * TILES, D])
        xlnT = sb("xlnT", [P, CHUNKS, KD, N])
        kT = sb("kT", [P, KD, N])
        ksq = sb("ksq", [P, KD, N])
        qT = sb("qT", [P, KD, N])
        qsq = sb("qsq", [P, KD, N])
        kn = sb("kn", [P, 2 * HPH * TILES])
        v = sb("v", [P, 2, TILES, D])
        kphi = sb("kphi", [P, RING, KD, HPH * M])
        ksum = sb("ksum", [P, KD * HPH * M])
        vsum = sb("vsum", [P, D])
        qphi = sb("qphi", [P, CHUNKS, PAIRS, N])
        kvm = sb("kvm", [P, 2 * KD, P])
        kvr = sb("kvr", [P, 2 * KD])
        kvb = sb("kvb", [P, 2 * KD])
        kvs = sb("kvs", [P, 2 * KD, P])
        den = sb("den", [P, 2, N])
        rden = sb("rden", [P, 2, N])
        att = sb("att", [P, CHUNKS, KD, N])
        pT = sb("pT", [RANK, N])
        gT = sb("gT", [P, FT, N])
        uT = sb("uT", [RANK, 2, N])
        fin = sb("fin", [P, CHUNKS * TILES, D])

        ps = ctx.enter_context(nc.psum_tensor("ps", [P, 8, 512], F32))

        weights_in = sem("weights_in")
        orf_in = sem("orf_in")
        ids_in = sem("ids_in")
        x_in = [sem(f"x_in{c}") for c in range(CHUNKS)]
        txt_in = sem("txt_in")
        orf_zeroed, consts_set, orf_scaled = sem("orf_zeroed"), sem("consts_set"), sem("orf_scaled")
        ids_safe, txt_gathered, txt_masked = sem("ids_safe"), sem("txt_gathered"), sem("txt_masked")
        xT_turned, xT_dve, xT_act = sem("xT_turned"), sem("xT_dve"), sem("xT_act")
        tok_done, tanh_done, energy_done = sem("tok_done"), sem("tanh_done"), sem("energy_done")
        logit_ready, expw_done, h_ready = sem("logit_ready"), sem("expw_done"), sem("h_ready")
        var_ready, rstd_ready, xln_ready = sem("var_ready"), sem("rstd_ready"), sem("xln_ready")
        xlnT_turned, xlnT_dve, xlnT_act = sem("xlnT_turned"), sem("xlnT_dve"), sem("xlnT_act")
        k_done, k_ready, ksq_ready = sem("k_done"), sem("k_ready"), sem("ksq_ready")
        q_done, q_ready, qsq_ready = sem("q_done"), sem("q_ready"), sem("qsq_ready")
        v_done, v_ready = sem("v_done"), sem("v_ready")
        kn_done, kn_ready = sem("kn_done"), sem("kn_ready")
        kproj_done, karg_ready, kphi_ready = sem("kproj_done"), sem("karg_ready"), sem("kphi_ready")
        qproj_done, qphi_ready = sem("qproj_done"), sem("qphi_ready")
        kv_done, sums_ready, kvall_done = sem("kv_done"), sem("sums_ready"), sem("kvall_done")
        kvm_ready, kvT_turned, kvs_ready = sem("kvm_ready"), sem("kvT_turned"), sem("kvs_ready")
        nd_done, den_ready, att_ready = sem("nd_done"), sem("den_ready"), sem("att_ready")
        hb_ready, wo_done, h2_ready = sem("hb_ready"), sem("wo_done"), sem("h2_ready")
        p_done, p_ready, ff_done, gelu_ready = sem("p_done"), sem("p_ready"), sem("ff_done"), sem("gelu_ready")
        u_done, u_ready, y_done, fin_ready = sem("u_done"), sem("u_ready"), sem("y_done"), sem("fin_ready")
        h2b_ready = sem("h2b_ready")
        out_stored = sem("out_stored")
        dve_step, pool_step = sem("dve_step"), sem("pool_step")

        G = CHUNKS * TILES

        loads = [
            (idn[:], ident), (w1[:], W1.rearrange("(k p) n -> p k n", p=P)), (b1c[:], b1t), (w2[:], W2), (b2c[:], b2t),
            (wk[:], WkT.rearrange("(k p) n -> p k n", p=P)), (bkc[:], bk), (wv[:], WvT.rearrange("(k p) n -> p k n", p=P)),
            (bvr[:], bv), (wq[:], WqT.rearrange("(k p) n -> p k n", p=P)), (bqc[:], bq), (nblk[:], norm_block),
            (ncol[:], norm_cols), (mask[:], head_mask), (wo[:], WoT.rearrange("(k p) n -> p k n", p=P)), (bor[:], bo),
            (u1[:], U1.rearrange("(k p) n -> p k n", p=P)), (v1[:], V1), (b1r[:], b1f),
            (u2[:], U2.rearrange("(k p) n -> p k n", p=P)), (v2[:], V2), (b2r[:], b2f),
        ]
        ALL_LOADS = 16 * len(loads)

        block = ctx.enter_context(nc.Block())

        @block.sync
        def _(sp):
            sp.dma_start(ids[:], x_txt).then_inc(ids_in, 16)

            def load_x(b):
                for c in range(CHUNKS):
                    t0 = c * N
                    sp.dma_start(xh[:, c * TILES:c * TILES + 2, :],
                                 x[b, 0, t0:t0 + 2 * P, :].rearrange("(t p) d -> p t d", p=P)).then_inc(x_in[c], 16)
                    rows = ROWS[2] if c < CHUNKS - 1 else TXT0
                    sp.dma_start(xh[0:rows, c * TILES + 2, :],
                                 x[b, 0, t0 + 2 * P:t0 + 2 * P + rows, :]).then_inc(x_in[c], 16)

            for b in range(B):
                if b > 0:
                    sp.wait_ge(h_ready, CHUNKS * b)
                load_x(b)
                sp.wait_ge(txt_masked, B)
                sp.dma_start(xh[TXT0:TXT0 + TXT, G - 1, :], txt[:, b, :]).then_inc(txt_in, 16)

        @block.gpsimd
        def _(pool):
            nc.gpsimd.memset(orf[:], 0.0).then_inc(orf_zeroed, 1)
            nc.gpsimd.memset(ones[:], 1.0)
            nc.gpsimd.memset(epsm[:], KERNEL_EPS)
            nc.gpsimd.memset(mhalf[:], -0.5)
            nc.gpsimd.memset(neps[:], NORM_EPS)
            nc.gpsimd.memset(hT[:], 0.0)
            nc.gpsimd.memset(kn[:], 0.0).then_inc(consts_set, 1)
            pool.wait_ge(ids_safe, 1)
            for i in range(B):
                nc.gpsimd.indirect_dma_start(
                    out=txt[:, i, :], out_offset=None, in_=emb,
                    in_offset=bass.IndirectOffsetOnAxis(ap=idu[:, i:i + 1], axis=0)).then_inc(txt_gathered, 16)

            POOL_STEPS = 2 * CHUNKS
            step = [0]

            def rstd(b, c, which):
                cols = slice(c * TILES, (c + 1) * TILES)
                pool.wait_ge(var_ready, (2 * b + which) * CHUNKS + c + 1)
                nc.gpsimd.tensor_tensor(ve[:, cols], mv[:, cols, 1], neps[:], ALU.add).then_inc(pool_step, 1)
                step[0] += 1
                pool.wait_ge(pool_step, b * POOL_STEPS + step[0])
                nc.gpsimd.tensor_tensor(rs[:, cols], ve[:, cols], mhalf[:], ALU.pow).then_inc(rstd_ready, 1)

            with pool.Fori(0, B) as b:
                step[0] = 0
                for c in range(CHUNKS):
                    rstd(b, c, 0)
                pool.wait_ge(weights_in, ALL_LOADS)
                for g in range(G):
                    r = ROWS[g % TILES]
                    pool.wait_ge(h_ready, CHUNKS * b + g // TILES + 1)
                    nc.gpsimd.tensor_tensor(hb[0:r, g, :], h[0:r, g, :], bor[0:r, :], ALU.add).then_inc(hb_ready, 1)
                for g in range(G):
                    c, t = divmod(g, TILES)
                    r = ROWS[t]
                    pool.wait_ge(kphi_ready, b * 2 * G + 2 * g + 2)
                    pool.wait_ge(v_ready, b * G + g + 1)
                    if g == 1:
                        nc.gpsimd.tensor_tensor(ksum[:], kphi[:, 0].rearrange("p k m -> p (k m)"),
                                                kphi[:, 1].rearrange("p k m -> p (k m)"), ALU.add)
                        nc.gpsimd.tensor_tensor(vsum[:], v[:, 0, 0, :], v[:, 0, 1, :], ALU.add).then_inc(sums_ready, 2)
                    elif g > 1:
                        pool.wait_ge(sums_ready, b * G + g)
                        nc.gpsimd.tensor_tensor(ksum[0:r, :], ksum[0:r, :], kphi[0:r, g % RING].rearrange("p k m -> p (k m)"), ALU.add)
                        nc.gpsimd.tensor_tensor(vsum[0:r, :], vsum[0:r, :], v[0:r, c % 2, t, :], ALU.add).then_inc(sums_ready, 1)
                for c in range(CHUNKS):
                    rstd(b, c, 1)
                    for t in range(TILES):
                        g, r = c * TILES + t, ROWS[t]
                        pool.wait_ge(h2_ready, b * G + g + 1)
                        pool.wait_ge(xln_ready, (2 * b + 1) * CHUNKS + c + 1)
                        nc.gpsimd.tensor_tensor(hb[0:r, g, :], h[0:r, g, :], b2r[0:r, :], ALU.add).then_inc(h2b_ready, 1)
                assert step[0] == POOL_STEPS
                for c in range(CHUNKS):
                    pool.wait_ge(fin_ready, b * G + (c + 1) * TILES)
                    t0 = c * N
                    pool.dma_start(out[b, t0:t0 + 2 * P, :].rearrange("(t p) d -> p t d", p=P),
                                   fin[:, c * TILES:c * TILES + 2, :]).then_inc(out_stored, 16)
                    pool.dma_start(out[b, t0 + 2 * P:t0 + N, :], fin[0:ROWS[2], c * TILES + 2, :]).then_inc(out_stored, 16)
            pool.wait_ge(out_stored, 16 * 2 * CHUNKS * B)

        @block.scalar
        def _(act):
            for dst, src in loads:
                act.dma_start(dst, src).then_inc(weights_in, 16)
            act.wait_ge(orf_zeroed, 1)
            for i in range(HPH):
                act.dma_start(orf[DK * i:DK * i + DK, M * i:M * i + M], orfT).then_inc(orf_in, 16)
            act.wait_ge(weights_in, ALL_LOADS)

            with act.Fori(0, B) as b:
                for c in range(CHUNKS):
                    act.wait_ge(xT_turned, b * 2 * CHUNKS + 2 * c + 2)
                    if c >= 2:
                        act.wait_ge(tok_done, b * CHUNKS + c - 1)
                    nc.scalar.activation(xT[:, c % 2, 1, :], ps[:, 1, 0:N], ACT.Copy).then_inc(xT_act, 1)
                    act.wait_ge(tok_done, b * CHUNKS + c + 1)
                    if c >= 2:
                        act.wait_ge(energy_done, b * CHUNKS + c - 1)
                    nc.scalar.activation(hT[:, c % 2, 0:N], ps[:, 2 + c % 2, 0:N], ACT.Tanh, bias=b1c[:]).then_inc(tanh_done, 1)
                    act.wait_ge(logit_ready, b * CHUNKS + c + 1)
                    nc.scalar.activation(lg[:, 3, c * TILES:(c + 1) * TILES], lg[:, 2, c * TILES:(c + 1) * TILES],
                                         ACT.Exp).then_inc(expw_done, 1)
                for c in range(CHUNKS):
                    act.wait_ge(xlnT_turned, (4 * b) * CHUNKS + 2 * c + 2)
                    nc.scalar.activation(xlnT[:, c, 1, :], ps[:, 5, 0:N], ACT.Copy).then_inc(xlnT_act, 1)
                for c in range(CHUNKS):
                    for hh in range(KD):
                        act.wait_ge(k_ready, (b * CHUNKS + c) * KD + hh + 1)
                        if c >= 1:
                            act.wait_ge(kn_done, b * CHUNKS + c)
                        nc.scalar.activation(ksq[:, hh, :], kT[:, hh, :], ACT.Square).then_inc(ksq_ready, 1)
                    for hh in range(KD):
                        act.wait_ge(q_ready, (b * CHUNKS + c) * KD + hh + 1)
                        if c >= 1:
                            act.wait_ge(qproj_done, (b * CHUNKS + c) * PAIRS)
                        nc.scalar.activation(qsq[:, hh, :], qT[:, hh, :], ACT.Square).then_inc(qsq_ready, 1)

                    def exp_k(t):
                        for hh in range(KD):
                            g = c * TILES + t
                            act.wait_ge(karg_ready, (b * G + g) * KD + hh + 1)
                            nc.scalar.activation(kphi[0:ROWS[t], g % RING, hh, :], kphi[0:ROWS[t], g % RING, hh, :],
                                                 ACT.Exp).then_inc(kphi_ready, 1)

                    def exp_q(p):
                        act.wait_ge(qproj_done, (b * CHUNKS + c) * PAIRS + p + 1)
                        nc.scalar.activation(qphi[:, c, p, :], ps[:, p % 2, 0:N], ACT.Exp).then_inc(qphi_ready, 1)

                    exp_k(0)
                    exp_q(0)
                    exp_q(1)
                    exp_k(1)
                    exp_q(2)
                    exp_q(3)
                    exp_k(2)
                    for p in range(4, PAIRS):
                        exp_q(p)
                for c in range(CHUNKS):
                    for hh in range(KD):
                        act.wait_ge(kvs_ready, b + 1)
                        act.wait_ge(nd_done, (b * CHUNKS + c) * KD + hh + 1)
                        if c >= 1:
                            act.wait_ge(att_ready, (b * CHUNKS + c - 1) * KD + hh + 1)
                        nc.scalar.activation(den[:, hh, :], ps[:, 2 * hh + 1, 0:N], ACT.Identity,
                                             bias=kvb[:, KD + hh:KD + hh + 1]).then_inc(den_ready, 1)
                for c in range(CHUNKS):
                    act.wait_ge(xlnT_turned, (4 * b + 2) * CHUNKS + 2 * c + 2)
                    nc.scalar.activation(xlnT[:, c, 1, :], ps[:, 7, 0:N], ACT.Copy).then_inc(xlnT_act, 1)
                for c in range(CHUNKS):
                    act.wait_ge(p_done, b * CHUNKS + c + 1)
                    if c >= 1:
                        act.wait_ge(ff_done, (b * CHUNKS + c) * FT)
                    nc.scalar.activation(pT[:], ps[0:RANK, 0, 0:N], ACT.Copy).then_inc(p_ready, 1)
                    for f in range(FT):
                        act.wait_ge(ff_done, (b * CHUNKS + c) * FT + f + 1)
                        if c >= 1 and f == 0:
                            act.wait_ge(u_done, b * CHUNKS + c)
                        nc.scalar.activation(gT[:, f, :], ps[:, 2 + f % 4, 0:N], ACT.Gelu_apprx_tanh,
                                             bias=b1r[:, f:f + 1]).then_inc(gelu_ready, 1)

        DVE_STEPS = 30

        @block.vector
        def _(dve):
            step = [0]

            def then(ins, b):
                ins.then_inc(dve_step, 1)
                step[0] += 1
                dve.wait_ge(dve_step, b * DVE_STEPS + step[0] if step[0] else 0)

            PRE = 6
            dve.wait_ge(ids_in, 16)
            pre = [0]

            def pre_then(ins):
                ins.then_inc(dve_step, 1)
                pre[0] += 1
                dve.wait_ge(dve_step, pre[0])

            pre_then(nc.vector.tensor_copy(idf[:], ids[:]))
            pre_then(nc.vector.tensor_scalar(idc[:], idf[:], 0.0, float(VOCAB - 1), ALU.max, ALU.min))
            nc.vector.tensor_copy(idu[:], idc[:]).then_inc(ids_safe, 1)
            pre_then(nc.vector.tensor_scalar(idle[:], idf[:], float(VOCAB - 1), None, ALU.is_le))
            pre_then(nc.vector.tensor_scalar(idok[:], idf[:], 0.0, None, ALU.is_ge))
            pre_then(nc.vector.tensor_tensor(idok[:], idok[:], idle[:], ALU.mult))
            dve.wait_ge(orf_in, 16 * HPH)
            pre_then(nc.vector.tensor_scalar(orf[:], orf[:], float(DK) ** -0.25, None, ALU.mult))
            nc.vector.memset(lg[:, 0, 0:1], 0.0).then_inc(orf_scaled, 1)
            dve.wait_ge(txt_gathered, 16 * B)
            for i in range(B):
                nc.vector.tensor_scalar(txt[:, i, :], txt[:, i, :], idok[:, i:i + 1], None, ALU.mult).then_inc(txt_masked, 1)
            assert pre[0] == PRE
            dve.wait_ge(weights_in, ALL_LOADS)
            dve.wait_ge(consts_set, 1)

            def norm(b, c, which):
                for t in range(TILES):
                    g, r = c * TILES + t, ROWS[t]
                    ins = nc.vector.bn_stats(st[0:r, g, :], h[0:r, g, :])
                then2(ins, b)
                nc.vector.memset(mv[ROWS[2]:P, c * TILES + 2, :], 1.0)
                for t in range(TILES):
                    g, r = c * TILES + t, ROWS[t]
                    ins = nc.vector.bn_aggr(mv[0:r, g, :], st[0:r, g, :])
                ins.then_inc(var_ready, 1)

            def scale(b, c, which):
                dve.wait_ge(rstd_ready, (2 * b + which) * CHUNKS + c + 1)
                if which == 1:
                    pass
                for t in range(TILES):
                    g, r = c * TILES + t, ROWS[t]
                    ins = nc.vector.tensor_scalar(xln[0:r, g, :], h[0:r, g, :], mv[0:r, g, 0:1], rs[0:r, g:g + 1],
                                                  ALU.subtract, ALU.mult)
                ins.then_inc(xln_ready, 1)

            def then2(ins, b):
                ins.then_inc(dve_step, 1)
                step[0] += 1
                dve.wait_ge(dve_step, PRE + b * DVE_STEPS + step[0])

            with dve.Fori(0, B) as b:
                step[0] = 0
                for c in range(CHUNKS):
                    cols = slice(c * TILES, (c + 1) * TILES)
                    dve.wait_ge(xT_turned, b * 2 * CHUNKS + 2 * c + 1)
                    if c >= 2:
                        dve.wait_ge(tok_done, b * CHUNKS + c - 1)
                    nc.vector.tensor_copy(xT[:, c % 2, 0, :], ps[:, 0, 0:N]).then_inc(xT_dve, 1)
                    dve.wait_ge(energy_done, b * CHUNKS + c + 1)
                    then2(nc.vector.tensor_scalar(lg[:, 0, cols], ps[:, 6, cols], b2c[:, 0:1], None, ALU.add), b)
                    one = lg[:, 0, cols].rearrange("p (t o) -> p t o", o=1)
                    then2(nc.vector.tensor_reduce(lg[:, 1, cols], one, AX.X, ALU.max), b)
                    nc.vector.tensor_tensor(lg[:, 2, cols], lg[:, 0, cols], lg[:, 1, cols], ALU.subtract).then_inc(logit_ready, 1)
                    dve.wait_ge(expw_done, b * CHUNKS + c + 1)
                    then2(nc.vector.tensor_reduce(lg[:, 4, cols], lg[:, 3, cols].rearrange("p (t o) -> p t o", o=1),
                                                  AX.X, ALU.add), b)
                    then2(nc.vector.reciprocal(lg[:, 4, cols], lg[:, 4, cols]), b)
                    then2(nc.vector.tensor_tensor(lg[:, 5, cols], lg[:, 3, cols], lg[:, 4, cols], ALU.mult), b)
                    if c == CHUNKS - 1:
                        then2(nc.vector.memset(lg[TXT0:TXT0 + TXT, 5, G - 1:G], 1.0), b)
                    for t in range(TILES):
                        g, r = c * TILES + t, ROWS[t]
                        ins = nc.vector.tensor_scalar(h[0:r, g, :], xh[0:r, g, :], lg[0:r, 5, g:g + 1], None, ALU.mult)
                    ins.then_inc(h_ready, 1)
                    dve.wait_ge(h_ready, b * CHUNKS + c + 1)
                    norm(b, c, 0)
                for c in range(CHUNKS):
                    scale(b, c, 0)
                for c in range(CHUNKS):
                    dve.wait_ge(xlnT_turned, (4 * b) * CHUNKS + 2 * c + 1)
                    nc.vector.tensor_copy(xlnT[:, c, 0, :], ps[:, 4, 0:N]).then_inc(xlnT_dve, 1)
                for c in range(CHUNKS):
                    for hh in range(KD):
                        dve.wait_ge(k_done, (b * CHUNKS + c) * KD + hh + 1)
                        if c >= 1:
                            dve.wait_ge(kproj_done, (b * CHUNKS + c) * TILES * KD)
                        nc.vector.tensor_scalar(kT[:, hh, :], ps[:, 2 + hh, 0:N], bkc[:, hh:hh + 1], None,
                                                ALU.add).then_inc(k_ready, 1)
                    for t in range(TILES):
                        g, r = c * TILES + t, ROWS[t]
                        dve.wait_ge(v_done, b * G + g + 1)
                        if c >= 2:
                            dve.wait_ge(kv_done, b * G + g - 2 * TILES + 1)
                            dve.wait_ge(sums_ready, b * G + g - 2 * TILES + 1)
                        nc.vector.tensor_tensor(v[0:r, c % 2, t, :], ps[0:r, 4 + g % 2, 0:D], bvr[0:r, :],
                                                ALU.add).then_inc(v_ready, 1)
                    dve.wait_ge(kn_done, b * CHUNKS + c + 1)
                    nc.vector.tensor_copy(kn[:, 0:2 * 2 * HPH], ps[:, 0, 0:4 * HPH])
                    nc.vector.tensor_copy(kn[0:ROWS[2], 4 * HPH:], ps[0:ROWS[2], 0, 4 * HPH:6 * HPH]).then_inc(kn_ready, 1)
                    for hh in range(KD):
                        dve.wait_ge(q_done, (b * CHUNKS + c) * KD + hh + 1)
                        if c >= 1:
                            dve.wait_ge(qproj_done, (b * CHUNKS + c) * PAIRS)
                        nc.vector.tensor_scalar(qT[:, hh, :], ps[:, 2 + hh, 0:N], bqc[:, hh:hh + 1], None,
                                                ALU.add).then_inc(q_ready, 1)
                    dve.wait_ge(kn_ready, b * CHUNKS + c + 1)
                    for t in range(TILES):
                        g, r = c * TILES + t, ROWS[t]
                        for hh in range(KD):
                            dve.wait_ge(kproj_done, (b * G + g) * KD + hh + 1)
                            if g >= RING:
                                dve.wait_ge(kv_done, b * G + g - RING + 1)
                                dve.wait_ge(sums_ready, b * G + g - RING + 1)
                            nrm = kn[0:r, (2 * t + hh) * HPH:(2 * t + hh + 1) * HPH].rearrange("p (i o) -> p i o", o=1)
                            nc.vector.tensor_tensor(kphi[0:r, g % RING, hh, :].rearrange("p (i m) -> p i m", m=M),
                                                    ps[0:r, 4 + hh, :].rearrange("p (i m) -> p i m", m=M),
                                                    nrm.to_broadcast([r, HPH, M]), ALU.subtract).then_inc(karg_ready, 1)
                dve.wait_ge(kvall_done, b + 1)
                for hh in range(KD):
                    nc.vector.tensor_tensor(kvm[:, hh, :], ps[:, 6 + hh, 0:P], mask[:], ALU.mult)
                    ins = nc.vector.scalar_tensor_tensor(out=kvm[:, KD + hh, :], in0=ps[:, 6 + hh, P:2 * P],
                                                         scalar=KERNEL_EPS * L, in1=mask[:], op0=ALU.add, op1=ALU.mult)
                ins.then_inc(kvm_ready, 1)
                dve.wait_ge(kvm_ready, b + 1)
                then2(nc.vector.tensor_reduce(kvr[:], kvm[:], AX.X, ALU.add), b)
                then2(nc.vector.tensor_scalar(kvb[:], kvr[:], KERNEL_EPS, None, ALU.mult), b)
                dve.wait_ge(kvT_turned, b + 1)
                nc.vector.tensor_copy(kvs[:].rearrange("p a m -> p (a m)"), ps[:, 5, :]).then_inc(kvs_ready, 1)

                def attend(c):
                    for hh in range(KD):
                        dve.wait_ge(den_ready, (b * CHUNKS + c) * KD + hh + 1)
                        then2(nc.vector.reciprocal(rden[:, hh, :], den[:, hh, :]), b)
                        nc.vector.scalar_tensor_tensor(out=att[:, c, hh, :], in0=ps[:, 2 * hh, 0:N], scalar=kvb[:, hh:hh + 1],
                                                       in1=rden[:, hh, :], op0=ALU.add, op1=ALU.mult).then_inc(att_ready, 1)

                def residual(c):
                    dve.wait_ge(hb_ready, (b + 1) * G)
                    for t in range(TILES):
                        g, r = c * TILES + t, ROWS[t]
                        dve.wait_ge(wo_done, b * G + g + 1)
                        nc.vector.tensor_tensor(h[0:r, g, :], ps[0:r, 4 + g % 2, 0:D], hb[0:r, g, :], ALU.add).then_inc(h2_ready, 1)
                    dve.wait_ge(h2_ready, b * G + (c + 1) * TILES)
                    norm(b, c, 1)

                for c in range(CHUNKS):
                    attend(c)
                    residual(c)
                for c in range(CHUNKS):
                    scale(b, c, 1)
                for c in range(CHUNKS):
                    dve.wait_ge(xlnT_turned, (4 * b + 2) * CHUNKS + 2 * c + 1)
                    nc.vector.tensor_copy(xlnT[:, c, 0, :], ps[:, 6, 0:N]).then_inc(xlnT_dve, 1)
                for c in range(CHUNKS):
                    dve.wait_ge(u_done, b * CHUNKS + c + 1)
                    nc.vector.tensor_copy(uT[:, c % 2, :], ps[0:RANK, 1, 0:N]).then_inc(u_ready, 1)
                    dve.wait_ge(h2b_ready, b * G + (c + 1) * TILES)
                    for t in range(TILES):
                        g, r = c * TILES + t, ROWS[t]
                        dve.wait_ge(y_done, b * G + g + 1)
                        nc.vector.tensor_tensor(fin[0:r, g, :], ps[0:r, 6 + g % 2, 0:D], hb[0:r, g, :], ALU.add).then_inc(fin_ready, 1)
                dve.wait_ge(out_stored, (b + 1) * 16 * 2 * CHUNKS)
                assert step[0] == DVE_STEPS, step[0]

        @block.tensor
        def _(pe):
            pe.wait_ge(weights_in, ALL_LOADS)
            pe.wait_ge(consts_set, 1)
            pe.wait_ge(orf_scaled, 1)

            def cols(t):
                return slice(t * P, t * P + ROWS[t])

            with pe.Fori(0, B) as b:
                for c in range(CHUNKS):
                    pe.wait_ge(x_in[c], 32 * b + 32)
                    if c == CHUNKS - 1:
                        pe.wait_ge(txt_in, 16 * b + 16)
                    if c >= 1:
                        pe.wait_ge(xT_dve, b * CHUNKS + c)
                        pe.wait_ge(xT_act, b * CHUNKS + c)
                    for k in range(KD):
                        for t in range(TILES):
                            g, r = c * TILES + t, ROWS[t]
                            ins = nc.tensor.transpose(ps[:, k, cols(t)], xh[0:r, g, k * P:(k + 1) * P], idn[0:r, 0:r])
                        ins.then_inc(xT_turned, 1)
                    if c >= 2:
                        pe.wait_ge(tanh_done, b * CHUNKS + c - 1)
                    pe.wait_ge(xT_dve, b * CHUNKS + c + 1)
                    pe.wait_ge(xT_act, b * CHUNKS + c + 1)
                    for k in range(KD):
                        ins = nc.tensor.matmul(ps[:, 2 + c % 2, 0:N], w1[:, k, :], xT[:, c % 2, k, :], start=k == 0, stop=k == KD - 1)
                    ins.then_inc(tok_done, 1)
                    pe.wait_ge(tanh_done, b * CHUNKS + c + 1)
                    if c >= 1:
                        pe.wait_ge(logit_ready, b * CHUNKS + c)
                    for t in range(TILES):
                        g = c * TILES + t
                        ins = nc.tensor.matmul(ps[:, 6, g:g + 1], hT[:, c % 2, t * P:(t + 1) * P], w2[:], start=True, stop=True)
                    ins.then_inc(energy_done, 1)

                def turn(c, which, bank):
                    pe.wait_ge(xln_ready, (2 * b + which) * CHUNKS + c + 1)
                    if c >= 1:
                        pe.wait_ge(xlnT_dve, (2 * b + which) * CHUNKS + c)
                        pe.wait_ge(xlnT_act, (2 * b + which) * CHUNKS + c)
                    for k in range(KD):
                        for t in range(TILES):
                            g, r = c * TILES + t, ROWS[t]
                            ins = nc.tensor.transpose(ps[:, bank + k, cols(t)], xln[0:r, g, k * P:(k + 1) * P], idn[0:r, 0:r])
                        ins.then_inc(xlnT_turned, 1)

                for c in range(CHUNKS):
                    turn(c, 0, 4)

                for c in range(CHUNKS):
                    pe.wait_ge(xlnT_dve, 2 * b * CHUNKS + c + 1)
                    pe.wait_ge(xlnT_act, 2 * b * CHUNKS + c + 1)
                    if c >= 1:
                        pe.wait_ge(q_ready, (b * CHUNKS + c) * KD)
                    for hh in range(KD):
                        for k in range(KD):
                            ins = nc.tensor.matmul(ps[:, 2 + hh, 0:N], wk[:, k, hh * P:(hh + 1) * P], xlnT[:, c, k, :],
                                                   start=k == 0, stop=k == KD - 1)
                        ins.then_inc(k_done, 1)
                    for t in range(TILES):
                        g, r = c * TILES + t, ROWS[t]
                        if c == 0 and t == 0:
                            pe.wait_ge(xlnT_dve, (2 * b + 1) * CHUNKS)
                            pe.wait_ge(xlnT_act, (2 * b + 1) * CHUNKS)
                        elif t < 2:
                            pe.wait_ge(karg_ready, (b * G + c * TILES) * KD)
                        if t == 2:
                            pe.wait_ge(v_ready, b * G + g - 1)
                        for k in range(KD):
                            ins = nc.tensor.matmul(ps[0:r, 4 + g % 2, 0:D], xlnT[:, c, k, cols(t)], wv[:, k, :],
                                                   start=k == 0, stop=k == KD - 1)
                        ins.then_inc(v_done, 1)
                    pe.wait_ge(ksq_ready, (b * CHUNKS + c + 1) * KD)
                    if c >= 1:
                        pe.wait_ge(qphi_ready, (b * CHUNKS + c) * PAIRS - 1)
                    for t in range(TILES):
                        r = ROWS[t]
                        for hh in range(KD):
                            o = (2 * t + hh) * HPH
                            ins = nc.tensor.matmul(ps[0:r, 0, o:o + HPH], ksq[:, hh, cols(t)], ncol[:],
                                                   start=True, stop=True)
                    ins.then_inc(kn_done, 1)
                    pe.wait_ge(k_ready, (b * CHUNKS + c + 1) * KD)
                    for hh in range(KD):
                        for k in range(KD):
                            ins = nc.tensor.matmul(ps[:, 2 + hh, 0:N], wq[:, k, hh * P:(hh + 1) * P], xlnT[:, c, k, :],
                                                   start=k == 0, stop=k == KD - 1)
                        ins.then_inc(q_done, 1)

                    def kproj(t):
                        g, r = c * TILES + t, ROWS[t]
                        for hh in range(KD):
                            if t == 0:
                                pe.wait_ge(v_ready, b * G + (c + 1) * TILES)
                            else:
                                pe.wait_ge(karg_ready, (b * G + g - 1) * KD + hh + 1)
                            nc.tensor.matmul(ps[0:r, 4 + hh, :], kT[:, hh, cols(t)], orf[:], start=True,
                                             stop=True).then_inc(kproj_done, 1)

                    def qproj(p):
                        hh, j = divmod(p, PPH)
                        pe.wait_ge(q_ready, (b * CHUNKS + c) * KD + hh + 1)
                        pe.wait_ge(qsq_ready, (b * CHUNKS + c) * KD + hh + 1)
                        if p == 0:
                            pe.wait_ge(kn_ready, b * CHUNKS + c + 1)
                        if c > 0 or p >= 2:
                            pe.wait_ge(qphi_ready, (b * CHUNKS + c) * PAIRS + p - 1)
                        nc.tensor.matmul(ps[:, p % 2, 0:N], orf[:, j * P:(j + 1) * P], qT[:, hh, :], start=True, stop=False)
                        nc.tensor.matmul(ps[:, p % 2, 0:N], nblk[:, j * P:(j + 1) * P], qsq[:, hh, :], start=False,
                                         stop=True).then_inc(qproj_done, 1)

                    def kv(t):
                        g, r = c * TILES + t, ROWS[t]
                        pe.wait_ge(kphi_ready, (b * G + g + 1) * KD)
                        for p in range(PAIRS):
                            hh, j = divmod(p, PPH)
                            ins = nc.tensor.matmul(ps[32 * j:32 * j + 32, 6 + hh, 0:P], v[0:r, c % 2, t, 32 * p:32 * p + 32],
                                                   kphi[0:r, g % RING, hh, j * P:(j + 1) * P], start=g == 0, stop=False,
                                                   tile_position=(0, 32 * j), skip_group_check=True)
                        ins.then_inc(kv_done, 1)

                    kproj(0)
                    qproj(0)
                    qproj(1)
                    kproj(1)
                    qproj(2)
                    qproj(3)
                    kv(0)
                    kproj(2)
                    qproj(4)
                    qproj(5)
                    kv(1)
                    qproj(6)
                    qproj(7)
                    kv(2)

                pe.wait_ge(sums_ready, (b + 1) * G)
                for p in range(PAIRS):
                    hh, j = divmod(p, PPH)
                    nc.tensor.matmul(ps[32 * j:32 * j + 32, 6 + hh, 0:P], vsum[:, 32 * p:32 * p + 32], epsm[:],
                                     start=False, stop=True, tile_position=(0, 32 * j), skip_group_check=True)
                for p in range(PAIRS):
                    hh, j = divmod(p, PPH)
                    ins = nc.tensor.matmul(ps[32 * j:32 * j + 32, 6 + hh, P:2 * P], ones[:], ksum[:, p * P:(p + 1) * P],
                                           start=False, stop=True, tile_position=(0, 32 * j), skip_group_check=True)
                ins.then_inc(kvall_done, 1)
                pe.wait_ge(kvm_ready, b + 1)
                pe.wait_ge(karg_ready, (b + 1) * G * KD)
                for i in range(2 * KD):
                    ins = nc.tensor.transpose(ps[:, 5, i * P:(i + 1) * P], kvm[:, i, :], idn[:])
                ins.then_inc(kvT_turned, 1)

                def numden(c):
                    pe.wait_ge(kvs_ready, b + 1)
                    pe.wait_ge(qphi_ready, (b * CHUNKS + c + 1) * PAIRS)
                    for hh in range(KD):
                        if c == 0:
                            pe.wait_ge(qphi_ready, (b + 1) * CHUNKS * PAIRS)
                            pe.wait_ge(q_ready, (b + 1) * CHUNKS * KD)
                            pe.wait_ge(qsq_ready, (b + 1) * CHUNKS * KD)
                        else:
                            pe.wait_ge(att_ready, (b * CHUNKS + c - 1) * KD + hh + 1)
                        for part in range(2):
                            for j in range(PPH):
                                ins = nc.tensor.matmul(ps[32 * j:32 * j + 32, 2 * hh + part, 0:N],
                                                       kvs[:, part * KD + hh, 32 * j:32 * j + 32],
                                                       qphi[:, c, hh * PPH + j, :], start=True, stop=True,
                                                       tile_position=(0, 32 * j))
                        ins.then_inc(nd_done, 1)

                def project(c):
                    pe.wait_ge(att_ready, (b * CHUNKS + c + 1) * KD)
                    for t in range(TILES):
                        g, r = c * TILES + t, ROWS[t]
                        if g == 0:
                            pe.wait_ge(kvs_ready, b + 1)
                        elif g >= 2:
                            pe.wait_ge(h2_ready, b * G + g - 1)
                        for k in range(KD):
                            ins = nc.tensor.matmul(ps[0:r, 4 + g % 2, 0:D], att[:, c, k, cols(t)], wo[:, k, :],
                                                   start=k == 0, stop=k == KD - 1)
                        ins.then_inc(wo_done, 1)

                numden(0)
                for c in range(CHUNKS):
                    if c + 1 < CHUNKS:
                        numden(c + 1)
                    project(c)
                for c in range(CHUNKS):
                    turn(c, 1, 6)

                def down_in(c):
                    pe.wait_ge(xlnT_dve, (2 * b + 1) * CHUNKS + c + 1)
                    pe.wait_ge(xlnT_act, (2 * b + 1) * CHUNKS + c + 1)
                    if c >= 1:
                        pe.wait_ge(p_ready, b * CHUNKS + c)
                    for k in range(KD):
                        ins = nc.tensor.matmul(ps[0:RANK, 0, 0:N], u1[:, k, :], xlnT[:, c, k, :], start=k == 0, stop=k == KD - 1)
                    ins.then_inc(p_done, 1)

                def up(c):
                    pe.wait_ge(p_ready, b * CHUNKS + c + 1)
                    for f in range(FT):
                        if c == 0 and f < 4:
                            pe.wait_ge(h2_ready, (b + 1) * G)
                        else:
                            pe.wait_ge(gelu_ready, (b * CHUNKS + c) * FT + f - 3)
                        nc.tensor.matmul(ps[:, 2 + f % 4, 0:N], v1[:, f * P:(f + 1) * P], pT[:], start=True,
                                         stop=True).then_inc(ff_done, 1)

                def down(c):
                    if c >= 1:
                        pe.wait_ge(u_ready, b * CHUNKS + c)
                    for f in range(FT):
                        pe.wait_ge(gelu_ready, (b * CHUNKS + c) * FT + f + 1)
                        ins = nc.tensor.matmul(ps[0:RANK, 1, 0:N], u2[:, f, :], gT[:, f, :], start=f == 0, stop=f == FT - 1)
                    ins.then_inc(u_done, 1)

                def up_out(c):
                    pe.wait_ge(u_ready, b * CHUNKS + c + 1)
                    for t in range(TILES):
                        g, r = c * TILES + t, ROWS[t]
                        if g < 2:
                            pe.wait_ge(xlnT_dve, (2 * b + 2) * CHUNKS)
                            pe.wait_ge(xlnT_act, (2 * b + 2) * CHUNKS)
                        else:
                            pe.wait_ge(fin_ready, b * G + g - 1)
                        nc.tensor.matmul(ps[0:r, 6 + g % 2, 0:D], uT[:, c % 2, cols(t)], v2[:], start=True,
                                         stop=True).then_inc(y_done, 1)

                down_in(0)
                for c in range(CHUNKS):
                    up(c)
                    if c + 1 < CHUNKS:
                        down_in(c + 1)
                    down(c)
                    up_out(c)
                pe.wait_ge(fin_ready, (b + 1) * G)


_OUT = ((2, 1056, 256), "float32")


def kernel(**inputs):
    import numpy as np
    import concourse.bacc as bacc
    from concourse.bass_utils import run_bass_kernel_spmd

    def rows(a):
        return np.ascontiguousarray(np.broadcast_to(np.asarray(a)[None, :], (128, np.asarray(a).shape[0])))

    def columns(a):
        return np.ascontiguousarray(np.asarray(a).reshape(-1, 128).T)

    DK, M = 16, 64
    own = np.kron(np.eye(128 // DK), np.ones((DK, M)))
    cols = np.kron(np.eye(128 // DK), np.ones((DK, 1)))
    pair = np.kron(np.eye(2), np.ones((DK, M)))
    host = {
        "x": inputs["x"], "x_txt": np.asarray(inputs["x_txt"]).T,
        "W1": inputs["L0_tok_W1"], "b1t": columns(inputs["L0_tok_b1"]), "W2": inputs["L0_tok_W2"],
        "b2t": np.ascontiguousarray(np.broadcast_to(np.asarray(inputs["L0_tok_b2"])[None, :], (128, 1))),
        "emb": inputs["L0_txt_w"],
        "WqT": np.asarray(inputs["L0_attn_Wq"]).T, "bq": columns(inputs["L0_attn_bq"]),
        "WkT": np.asarray(inputs["L0_attn_Wk"]).T, "bk": columns(inputs["L0_attn_bk"]),
        "WvT": np.asarray(inputs["L0_attn_Wv"]).T, "bv": rows(inputs["L0_attn_bv"]),
        "WoT": np.asarray(inputs["L0_attn_Wo"]).T, "bo": rows(inputs["L0_attn_bo"]),
        "orfT": np.asarray(inputs["L0_attn_orf"]).T,
        "U1": inputs["L0_ffn_U1"], "V1": inputs["L0_ffn_V1"], "b1f": columns(inputs["L0_ffn_b1"]),
        "U2": inputs["L0_ffn_U2"], "V2": inputs["L0_ffn_V2"], "b2f": rows(inputs["L0_ffn_b2"]),
        "ident": np.eye(128, dtype=np.float32),
        "norm_block": (own * (-0.5 / DK ** 0.5)).astype(np.float32),
        "norm_cols": (cols * (0.5 / DK ** 0.5)).astype(np.float32),
        "head_mask": (np.tile(pair, (4, 1)) / M).astype(np.float32),
    }
    nc = bacc.Bacc("TRN2", target_bir_lowering=False, num_devices=1)
    arrays, args = {}, []
    for name, a in host.items():
        a = np.ascontiguousarray(a)
        arrays[f"in_{name}"] = a
        args.append(nc.dram_tensor(f"in_{name}", a.shape, mybir.dt.from_np(a.dtype), kind="ExternalInput").ap())
    args.append(nc.dram_tensor("out_0", _OUT[0], mybir.dt.float32, kind="ExternalOutput").ap())
    build(nc, *args)
    r = run_bass_kernel_spmd(nc, [arrays], core_ids=[0])
    return r.results[0]["out_0"]
```

```python
from contextlib import ExitStack

import concourse.bass as bass
from concourse import mybir

ALU = mybir.AluOpType
ACT = mybir.ActivationFunctionType
AX = mybir.AxisListType
F32 = mybir.dt.float32
F32R = mybir.dt.float32r
I32 = mybir.dt.int32
U32 = mybir.dt.uint32

P = 128
CHUNKS = 3
TILES = 3
BLK = 32
KERNEL_EPS = 1e-6
NORM_EPS = 1e-5

TOK_COLS = [("ident", 128), ("W1", 256), ("b1", 1), ("W2", 1), ("b2", 1)]
RAW_COLS = [("WkT", 512), ("WqT", 512), ("orf", 512), ("norm_block", 512), ("V1", 1024)]
ROW_COLS = [("WvT", 512), ("bv", 256), ("bo", 256), ("bk", 2), ("bq", 2)]
REST_COLS = [("norm_cols", 32), ("head_mask", 128), ("WoT", 512), ("U1", 256), ("U2", 512), ("V2", 256), ("b1f", 8), ("b2f", 256)]


def width(columns):
    return sum(n for _, n in columns)


def build(nc, x, ids_in_dram, emb, tok_w, raw_w, row_w, rest_w, out):
    B, _, X, D = x.shape
    TXT = ids_in_dram.shape[0]
    VOCAB = emb.shape[0]
    L = X + TXT
    N = L // CHUNKS
    ROWS = [P, P, N - 2 * P]
    TXT0 = ROWS[2] - TXT
    G = CHUNKS * TILES
    NC = B * CHUNKS
    KD = D // P
    DK, M = 16, 64
    HPH = P // DK
    PAIRS = D // DK // 2
    PPH = PAIRS // KD
    RANK, FF = 64, 1024
    FT = FF // P
    FORDER = [f // 2 + FT // 2 * (f % 2) for f in range(FT)]
    RING = 3
    NB = KD * N // BLK
    assert KD * P == D and 2 * M == P and PPH * 2 * DK == P and N <= 512 and 2 * RANK == P and N % BLK == 0

    ctx = ExitStack()
    with ctx:
        def sb(name, shape, dt=F32):
            return ctx.enter_context(nc.sbuf_tensor(name, shape, dt))

        def sem(name):
            return ctx.enter_context(nc.semaphore(name))

        tokw = sb("tokw", [P, width(TOK_COLS)])
        roww = sb("roww", [P, width(ROW_COLS)])
        restw = sb("restw", [P, width(REST_COLS)])
        work = sb("work", [P, CHUNKS, PAIRS, N])
        flat = work[:].rearrange("p c a n -> p (c a n)")

        def part(tile, columns, name):
            at = 0
            for n, wide in columns:
                if n == name:
                    return tile[:, at:at + wide]
                at += wide

        def halves(ap, k=KD):
            return ap.rearrange("p (k n) -> p k n", k=k)

        idn = part(tokw, TOK_COLS, "ident")
        w1 = halves(part(tokw, TOK_COLS, "W1"))
        b1c, w2, b2c = (part(tokw, TOK_COLS, n) for n in ("b1", "W2", "b2"))
        wv = halves(part(roww, ROW_COLS, "WvT"))
        bvr, bor, bkc, bqc = (part(roww, ROW_COLS, n) for n in ("bv", "bo", "bk", "bq"))
        wo = halves(part(restw, REST_COLS, "WoT"))
        u1 = halves(part(restw, REST_COLS, "U1"))
        u2 = halves(part(restw, REST_COLS, "U2"), FT)
        v2, b1f, b2r, ncol, mask = (part(restw, REST_COLS, n) for n in ("V2", "b1f", "b2f", "norm_cols", "head_mask"))
        raw = flat[:, 0:width(RAW_COLS)]
        at = width(RAW_COLS)
        xh = flat[:, at:at + G * D].rearrange("p (g d) -> p g d", d=D)
        at += G * D
        xT = flat[:, at:at + 2 * KD * N].rearrange("p (s k n) -> p s k n", s=2, k=KD)
        at += 2 * KD * N
        hT = flat[:, at:at + 2 * TILES * P].rearrange("p (s n) -> p s n", s=2)
        at += 2 * TILES * P
        txt = flat[0:TXT, at:at + B * D].rearrange("p (b d) -> p b d", b=B)
        assert at + B * D <= CHUNKS * PAIRS * N
        wk = sb("wk", [P, 2, KD, D], F32R)
        wq = sb("wq", [P, 2, KD, D], F32R)
        orf = sb("orf", [P, 2, HPH * M], F32R)
        nblk = sb("nblk", [P, HPH * M], F32R)
        v1 = sb("v1", [P, 2, FF], F32R)
        ones = sb("ones", [P, 2 * DK])
        epsm = sb("epsm", [P, P])
        mhalf = sb("mhalf", [P, TILES])
        neps = sb("neps", [P, TILES])
        ids = sb("ids", [TXT, B], I32)
        idf = sb("idf", [TXT, 4, B])
        idu = sb("idu", [TXT, B], U32)
        lg = sb("lg", [P, 6, G])
        hb = sb("hb", [P, B * G, D])
        xlnT = sb("xlnT", [P, NC + 1, KD, N])
        vs = [sb("v_cur", [P, G + 1, D]), sb("v_next", [P, G + 1, D])]
        st = sb("st", [P, G, 6])
        mv = sb("mv", [P, G, 2])
        ve = sb("ve", [P, G])
        nm, nmr = sb("nm", [P, TILES]), sb("nmr", [P, TILES])
        zero = sb("zero", [P, TILES])
        rs = sb("rs", [P, G])
        xln = sb("xln", [P, 2, TILES, D])
        xs = sb("xs", [P, 2, KD, N], F32R)
        ks = sb("ks", [P, 2, KD, N], F32R)
        qs = sb("qs", [P, 2, KD, N], F32R)
        sq = sb("sq", [P, KD, N])
        qsq = sb("qsq", [P, 2, KD, N], F32R)
        knT = sb("knT", [P, N])
        kn = sb("kn", [P, TILES, KD, HPH])
        kphi = sb("kphi", [P, RING, KD, HPH * M])
        ksum = sb("ksum", [P, KD * HPH * M])
        kvm = sb("kvm", [P, 2 * KD, P])
        kvr = sb("kvr", [P, 2, 2 * KD])
        kvs = sb("kvs", [P, 2 * KD, P])
        rden = sb("rden", [P, KD, N])
        rec = sb("rec", [P, NB, 2])
        att = sb("att", [P, CHUNKS, KD, N])
        h2 = sb("h2", [P, G, D])
        den = [kphi[:, c].rearrange("p k m -> p (k m)")[:, 0:KD * N] for c in range(CHUNKS)]
        xln2T = sb("xln2T", [P, KD, N])
        pS = sb("pS", [P, 2, N], F32R)
        uT = sb("uT", [P, N])

        ps = ctx.enter_context(nc.psum_tensor("ps", [P, 8, 512], F32))

        ids_loaded, tok_in, raw_in, row_in, rest_in = (sem(n) for n in ("ids_loaded", "tok_in", "raw_in", "row_in", "rest_in"))
        x_in = [sem(f"x_in{c}") for c in range(CHUNKS)]
        txt_in, consts_set = sem("txt_in"), sem("consts_set")
        ids_safe, txt_gathered, txt_masked = sem("ids_safe"), sem("txt_gathered"), sem("txt_masked")
        hi_split, lo_split = sem("hi_split"), sem("lo_split")
        xT_turned, xT_ready = sem("xT_turned"), sem("xT_ready")
        tok_done, tanh_done, energy_done = sem("tok_done"), sem("tanh_done"), sem("energy_done")
        logit_ready, expw_done, h_ready = sem("logit_ready"), sem("expw_done"), sem("h_ready")
        var_ready, rstd_ready, xln_ready = sem("var_ready"), sem("rstd_ready"), sem("xln_ready")
        xlnT_turned, xlnT_ready = sem("xlnT_turned"), sem("xlnT_ready")
        v_done, v_ready, vsum_ready, hb_ready = sem("v_done"), sem("v_ready"), sem("vsum_ready"), sem("hb_ready")
        xs_ready = sem("xs_ready")
        k_done, ksq_ready, k_ready = sem("k_done"), sem("ksq_ready"), sem("k_ready")
        q_done, qsq_made, q_ready, qsq_ready = sem("q_done"), sem("qsq_made"), sem("q_ready"), sem("qsq_ready")
        kn_done, knT_ready, kn_turned, kn_ready = sem("kn_done"), sem("knT_ready"), sem("kn_turned"), sem("kn_ready")
        kproj_done, karg_ready, kphi_ready = sem("kproj_done"), sem("karg_ready"), sem("kphi_ready")
        qproj_done, qphi_ready = sem("qproj_done"), sem("qphi_ready")
        kv_done, ksum_ready, kvall_done, v_moved = sem("kv_done"), sem("ksum_ready"), sem("kvall_done"), sem("v_moved")
        kvm_ready, kvT_turned, kvs_ready = sem("kvm_ready"), sem("kvT_turned"), sem("kvs_ready")
        nd_done, nd_ready, att_ready = sem("nd_done"), sem("nd_ready"), sem("att_ready")
        wo_done, h2_ready, h2b_ready = sem("wo_done"), sem("h2_ready"), sem("h2b_ready")
        var2_ready, rstd2_ready, xln2_ready = sem("var2_ready"), sem("rstd2_ready"), sem("xln2_ready")
        xln2T_turned, xln2T_ready = sem("xln2T_turned"), sem("xln2T_ready")
        p_done, phi_ready, p_ready, ff_done, gelu_ready = (sem(n) for n in ("p_done", "phi_ready", "p_ready", "ff_done", "gelu_ready"))
        u_done, u_ready, y_done = sem("u_done"), sem("u_ready"), sem("y_done")
        fin_ready, out_stored = sem("fin_ready"), sem("out_stored")
        dve_step, pool_step = sem("dve_step"), sem("pool_step")

        ND_BANKS = [(2, 4), (6, 2), (4, 6)]

        WO_BANKS = [0, 4, 0]

        def tile_cols(t):
            return slice(t * P, t * P + ROWS[t])

        block = ctx.enter_context(nc.Block())

        @block.sync
        def _(sp):
            def load_x(c):
                b, cc = divmod(c, CHUNKS)
                t0 = cc * N
                sp.dma_start(xh[:, cc * TILES:cc * TILES + 2, :],
                             x[b, 0, t0:t0 + 2 * P, :].rearrange("(t p) d -> p t d", p=P)).then_inc(x_in[cc], 16)
                rows = ROWS[2] if cc < CHUNKS - 1 else TXT0
                sp.dma_start(xh[0:rows, cc * TILES + 2, :],
                             x[b, 0, t0 + 2 * P:t0 + 2 * P + rows, :]).then_inc(x_in[cc], 16)
            load_x(0)
            sp.dma_start(ids[:], ids_in_dram).then_inc(ids_loaded, 16)
            load_x(1)
            load_x(2)
            sp.dma_start(raw, raw_w).then_inc(raw_in, 16)

            def load_txt(b):
                sp.dma_start(xh[TXT0:TXT0 + TXT, G - 1, :], txt[:, b, :]).then_inc(txt_in, 16)

            sp.wait_ge(txt_masked, B)
            load_txt(0)
            for c in range(CHUNKS, NC):
                sp.wait_ge(xln_ready, c - CHUNKS + 1)
                sp.wait_ge(hb_ready, (c - CHUNKS + 1) * TILES)
                load_x(c)
            load_txt(1)

            with sp.Fori(0, B) as b:
                sp.wait_ge(kvall_done, b + 1)
                sp.dma_start(vs[0][:], vs[1][:]).then_inc(v_moved, 16)
                for c in range(CHUNKS):
                    t0 = c * N
                    sp.wait_ge(fin_ready, b * G + (c + 1) * TILES + 1)
                    sp.dma_start(out[b, t0:t0 + 2 * P, :].rearrange("(t p) d -> p t d", p=P),
                                 h2[:, c * TILES:c * TILES + 2, :]).then_inc(out_stored, 16)
                    sp.dma_start(out[b, t0 + 2 * P:t0 + N, :], h2[0:ROWS[2], c * TILES + 2, :]).then_inc(out_stored, 16)
            sp.wait_ge(out_stored, B * 16 * 2 * CHUNKS + 1)
            sp.wait_ge(v_moved, B * 16)

        @block.gpsimd
        def _(pool):
            nc.gpsimd.memset(hT, 0.0)
            nc.gpsimd.memset(neps[:], NORM_EPS)
            nc.gpsimd.memset(mhalf[:], -0.5)
            nc.gpsimd.memset(zero[:], 0.0)
            nc.gpsimd.memset(mv[:], 1.0)
            nc.gpsimd.memset(ones[:], 1.0)
            nc.gpsimd.memset(knT[:], 0.0)
            nc.gpsimd.memset(xlnT[:, NC], 0.0)
            nc.gpsimd.memset(vs[0][:, G, :], 0.0)
            nc.gpsimd.memset(vs[1][:, G, :], 0.0)
            nc.gpsimd.memset(vs[0][:, 2:G:TILES, :], 0.0)
            nc.gpsimd.memset(vs[1][:, 2:G:TILES, :], 0.0)
            nc.gpsimd.memset(epsm[:], KERNEL_EPS).then_inc(consts_set, 1)
            nc.gpsimd.memset(rec[:], 1.0).then_inc(out_stored, 1)
            pool.wait_ge(ids_safe, 1)
            for i in range(B):
                nc.gpsimd.indirect_dma_start(
                    out=txt[:, i, :], out_offset=None, in_=emb,
                    in_offset=bass.IndirectOffsetOnAxis(ap=idu[:, i:i + 1], axis=0)).then_inc(txt_gathered, 16)
            steps = [0]

            def sum_v(c):
                b, cc = divmod(c, CHUNKS)
                for t in range(TILES):
                    g = cc * TILES + t
                    pool.wait_ge(v_ready, c * TILES + t + 1)
                    if g >= 1:
                        r = ROWS[t]
                        a = vs[b][0:r, 0, :] if g == 1 else vs[b][0:r, G, :]
                        if g >= 2:
                            pool.wait_ge(vsum_ready, b * (G - 1) + g - 1)
                        nc.gpsimd.tensor_tensor(vs[b][0:r, G, :], a, vs[b][0:r, g, :], ALU.add).then_inc(vsum_ready, 1)

            def split_lo(dst, src, hi, n):
                pool.wait_ge(hi_split, n)
                nc.gpsimd.tensor_tensor(dst, src, hi.bitcast(F32), ALU.subtract).then_inc(lo_split, 1)

            for c in range(NC):
                cols = slice(c % CHUNKS * TILES, (c % CHUNKS + 1) * TILES)
                pool.wait_ge(var_ready, c + 1)
                nc.gpsimd.tensor_tensor(ve[:, cols], mv[:, cols, 1], neps[:], ALU.add).then_inc(pool_step, 1)
                steps[0] += 1
                pool.wait_ge(pool_step, steps[0])
                nc.gpsimd.tensor_tensor(rs[:, cols], ve[:, cols], mhalf[:], ALU.pow).then_inc(rstd_ready, 1)
                if c == 0:
                    pool.wait_ge(row_in, 16)
                for t in range(TILES):
                    g, r = c % CHUNKS * TILES + t, ROWS[t]
                    nc.gpsimd.tensor_tensor(hb[0:r, c * TILES + t, :], xh[0:r, g, :], bor[0:r, :], ALU.add).then_inc(hb_ready, 1)
                if c == 0:
                    split_lo(wk[:, 1], halves(part(raw, RAW_COLS, "WkT")), wk[:, 0], 1)
                if c == 1:
                    split_lo(wq[:, 1], halves(part(raw, RAW_COLS, "WqT")), wq[:, 0], 2)
                if c == 2:
                    split_lo(v1[:, 1], part(raw, RAW_COLS, "V1"), v1[:, 0], 5)
                if c >= 2:
                    sum_v(c - 2)
            sum_v(NC - 2)
            sum_v(NC - 1)
            FIRST = steps[0]

            with pool.Fori(0, B) as b:
                for g in range(1, G):
                    r = ROWS[g % TILES]
                    pool.wait_ge(kphi_ready, b * KD * G + KD * (g + 1))
                    if g == 1:
                        nc.gpsimd.tensor_tensor(ksum[:], kphi[:, 0].rearrange("p k m -> p (k m)"),
                                                kphi[:, 1].rearrange("p k m -> p (k m)"), ALU.add).then_inc(ksum_ready, 2)
                    else:
                        pool.wait_ge(ksum_ready, b * G + g)
                        nc.gpsimd.tensor_tensor(ksum[0:r, :], ksum[0:r, :], kphi[0:r, g % RING].rearrange("p k m -> p (k m)"),
                                                ALU.add).then_inc(ksum_ready, 1)
                steps[0] = 0

                def rstd2(c):
                    cols = slice(c * TILES, (c + 1) * TILES)
                    pool.wait_ge(var2_ready, b * CHUNKS + c + 1)
                    nc.gpsimd.tensor_tensor(ve[:, cols], mv[:, cols, 1], neps[:], ALU.add).then_inc(pool_step, 1)
                    steps[0] += 1
                    pool.wait_ge(pool_step, FIRST + b * (CHUNKS + 2) + steps[0])
                    power = nc.gpsimd.tensor_tensor(rs[:, cols], ve[:, cols], mhalf[:], ALU.pow)
                    if c > 0:
                        power.then_inc(rstd2_ready, 1)
                        return
                    power.then_inc(pool_step, 1)
                    nc.gpsimd.tensor_tensor(nm[:], zero[:], mv[:, cols, 0], ALU.subtract).then_inc(pool_step, 1)
                    steps[0] += 2
                    pool.wait_ge(pool_step, FIRST + b * (CHUNKS + 2) + steps[0])
                    nc.gpsimd.tensor_tensor(nmr[:], nm[:], rs[:, cols], ALU.mult).then_inc(rstd2_ready, 1)

                def add_b2(c):
                    pool.wait_ge(xln2_ready, b * CHUNKS + c + 1)
                    for t in range(TILES):
                        g, r = c * TILES + t, ROWS[t]
                        nc.gpsimd.tensor_tensor(h2[0:r, g, :], h2[0:r, g, :], b2r[0:r, :], ALU.add).then_inc(h2b_ready, 1)

                for c in range(CHUNKS):
                    rstd2(c)
                for c in range(CHUNKS):
                    add_b2(c)

        @block.scalar
        def _(act):
            act.dma_start(tokw[:], tok_w).then_inc(tok_in, 16)
            act.dma_start(roww[:], row_w).then_inc(row_in, 16)
            act.dma_start(restw[:], rest_w).then_inc(rest_in, 16)
            act.wait_ge(tok_in, 16)
            act.wait_ge(consts_set, 1)

            def split_hi(c):
                if c == 0:
                    act.wait_ge(raw_in, 16)
                    nc.scalar.activation(wk[:, 0], halves(part(raw, RAW_COLS, "WkT")), ACT.Copy).then_inc(hi_split, 1)
                if c == 1:
                    nc.scalar.activation(wq[:, 0], halves(part(raw, RAW_COLS, "WqT")), ACT.Copy).then_inc(hi_split, 1)
                if c == 2:
                    nc.scalar.activation(orf[:, 0], part(raw, RAW_COLS, "orf"), ACT.Copy, scale=float(DK) ** -0.25).then_inc(hi_split, 1)
                    nc.scalar.activation(nblk[:], part(raw, RAW_COLS, "norm_block"), ACT.Copy).then_inc(hi_split, 1)
                    nc.scalar.activation(v1[:, 0], part(raw, RAW_COLS, "V1"), ACT.Copy).then_inc(hi_split, 1)

            def turn_x(c):
                act.wait_ge(xT_turned, c + 1)
                if c >= 2:
                    act.wait_ge(tok_done, c - 1)
                nc.scalar.activation(xT[:, c % 2], ps[:, 0:2, 0:N], ACT.Copy).then_inc(xT_ready, 1)

            def turn_xln(c):
                act.wait_ge(xlnT_turned, c + 1)
                nc.scalar.activation(xlnT[:, c], ps[:, 6:8, 0:N], ACT.Copy).then_inc(xlnT_ready, 1)

            turn_x(0)
            for c in range(NC):
                act.wait_ge(tok_done, c + 1)
                if c >= 2:
                    act.wait_ge(energy_done, c - 1)
                nc.scalar.activation(hT[:, c % 2, 0:N], ps[:, 2, 0:N], ACT.Tanh, bias=b1c).then_inc(tanh_done, 1)
                if c + 1 < NC:
                    turn_x(c + 1)
                act.wait_ge(logit_ready, c + 1)
                cols = slice(c % CHUNKS * TILES, (c % CHUNKS + 1) * TILES)
                nc.scalar.activation(lg[:, 3, cols], lg[:, 2, cols], ACT.Exp).then_inc(expw_done, 1)
                split_hi(c)
                if c >= 1:
                    turn_xln(c - 1)
            def keys(b, c, hh):
                act.wait_ge(k_done, (b * CHUNKS + c) * KD + hh + 1)
                if c >= 1:
                    act.wait_ge(kproj_done, (b * CHUNKS + c) * TILES * KD)
                    act.wait_ge(qsq_ready, (b * CHUNKS + c) * KD)
                nc.scalar.activation(ks[:, 0, hh, :], ps[:, 2 + hh, 0:N], ACT.Identity, bias=bkc[:, hh:hh + 1])
                nc.scalar.activation(sq[:, hh, :], ps[:, 2 + hh, 0:N], ACT.Square, bias=bkc[:, hh:hh + 1]).then_inc(ksq_ready, 1)

            def queries(b, c, hh):
                act.wait_ge(q_done, (b * CHUNKS + c) * KD + hh + 1)
                if c >= 1:
                    act.wait_ge(qproj_done, (b * CHUNKS + c - 1) * PAIRS + (hh + 1) * PPH)
                act.wait_ge(kn_done, b * CHUNKS + c + 1)
                nc.scalar.activation(qs[:, 0, hh, :], ps[:, 2 + hh, 0:N], ACT.Identity, bias=bqc[:, hh:hh + 1])
                nc.scalar.activation(sq[:, hh, :], ps[:, 2 + hh, 0:N], ACT.Square, bias=bqc[:, hh:hh + 1]).then_inc(qsq_made, 1)

            def norms(b, c):
                act.wait_ge(kn_done, b * CHUNKS + c + 1)
                nc.scalar.activation(knT[0:KD * BLK, :], ps[0:KD * BLK, 4, 0:N], ACT.Copy).then_inc(knT_ready, 1)

            keys(0, 0, 0)
            keys(0, 0, 1)
            turn_xln(NC - 1)
            norms(0, 0)
            queries(0, 0, 0)
            queries(0, 0, 1)
            act.wait_ge(rest_in, 16)

            with act.Fori(0, B) as b:
                def exp_k(c, t):
                    g = c * TILES + t
                    for hh in range(KD):
                        act.wait_ge(karg_ready, (b * G + g) * KD + hh + 1)
                        nc.scalar.activation(kphi[0:ROWS[t], g % RING, hh, :], kphi[0:ROWS[t], g % RING, hh, :],
                                             ACT.Exp).then_inc(kphi_ready, 1)

                def exp_q(c, p):
                    act.wait_ge(qproj_done, (b * CHUNKS + c) * PAIRS + p + 1)
                    nc.scalar.activation(work[:, c, p, :], ps[:, p % 2, 0:N], ACT.Exp).then_inc(qphi_ready, 1)

                def normaliser(c, hh):
                    act.wait_ge(nd_done, (b * CHUNKS + c) * KD + hh + 1)
                    bank = ND_BANKS[c][hh]
                    nc.scalar.activation(den[c][:, hh * N:(hh + 1) * N], ps[:, bank + 1, 0:N], ACT.Identity,
                                         bias=kvr[:, 1, KD + hh:KD + hh + 1])
                    nc.scalar.activation(att[:, c, hh, :], ps[:, bank, 0:N], ACT.Identity,
                                         bias=kvr[:, 1, hh:hh + 1]).then_inc(nd_ready, 1)

                def normalise_first():
                    act.wait_ge(rstd2_ready, b * CHUNKS + 1)
                    for t in range(TILES):
                        ins = nc.scalar.activation(xln[0:ROWS[t], 0, t, :], h2[0:ROWS[t], t, :], ACT.Identity,
                                                   scale=rs[0:ROWS[t], t:t + 1], bias=nmr[0:ROWS[t], t:t + 1])
                    ins.then_inc(xln2_ready, 1)

                def turn_xln2(c):
                    act.wait_ge(xln2T_turned, b * CHUNKS + c + 1)
                    nc.scalar.activation(xln2T[:], ps[:, 2:4, 0:N], ACT.Copy).then_inc(xln2T_ready, 1)

                def low_rank(c):
                    act.wait_ge(p_done, b * CHUNKS + c + 1)
                    nc.scalar.activation(pS[:, c % 2, :], ps[:, 2, 0:N], ACT.Copy).then_inc(phi_ready, 1)

                def gelu(c, i):
                    act.wait_ge(ff_done, (b * CHUNKS + c) * FT + i + 1)
                    nc.scalar.activation(work[:, c, i, :], ps[:, 4 + i % 4, 0:N], ACT.Gelu_apprx_tanh,
                                         bias=b1f[:, FORDER[i]:FORDER[i] + 1]).then_inc(gelu_ready, 1)

                for c in range(CHUNKS - 1):
                    exp_k(c, 0)
                    exp_q(c, 0)
                    exp_k(c, 1)
                    exp_q(c, 1)
                    exp_k(c, 2)
                    exp_q(c, 2)
                    exp_q(c, 3)
                    keys(b, c + 1, 0)
                    keys(b, c + 1, 1)
                    exp_q(c, 4)
                    exp_q(c, 5)
                    norms(b, c + 1)
                    exp_q(c, 6)
                    queries(b, c + 1, 0)
                    exp_q(c, 7)
                    queries(b, c + 1, 1)
                c = CHUNKS - 1
                exp_k(c, 0)
                exp_q(c, 0)
                exp_k(c, 1)
                exp_q(c, 1)
                exp_k(c, 2)
                for p in range(2, PAIRS - 1):
                    exp_q(c, p)
                act.wait_ge(kvs_ready, b + 1)
                normaliser(0, 0)
                normaliser(0, 1)
                exp_q(c, PAIRS - 1)
                normaliser(1, 0)
                normaliser(1, 1)
                normaliser(2, 0)
                normaliser(2, 1)
                normalise_first()
                turn_xln2(0)
                low_rank(0)
                for c in range(CHUNKS):
                    for i in range(4):
                        gelu(c, i)
                    if c + 1 < CHUNKS:
                        turn_xln2(c + 1)
                    gelu(c, 4)
                    gelu(c, 5)
                    if c + 1 < CHUNKS:
                        low_rank(c + 1)
                    gelu(c, 6)
                    gelu(c, 7)
                keys(b, CHUNKS, 0)
                keys(b, CHUNKS, 1)
                norms(b, CHUNKS)
                queries(b, CHUNKS, 0)
                queries(b, CHUNKS, 1)

        DVE_FIRST, DVE_STEPS = 44, 25

        @block.vector
        def _(dve):
            steps, base = [0], [0]

            def then(ins):
                ins.then_inc(dve_step, 1)
                steps[0] += 1
                dve.wait_ge(dve_step, base[0] + steps[0])

            def two_tiles(bank):
                return ps[:, bank, :].rearrange("p (t d) -> p t d", t=2)

            def twice(row):
                return row.rearrange("p (o d) -> p o d", o=1).to_broadcast([P, 2, D])

            f, c0, ok, le = (idf[:, i, :] for i in range(4))
            dve.wait_ge(ids_loaded, 16)
            then(nc.vector.tensor_copy(f, ids[:]))
            then(nc.vector.tensor_scalar(c0, f, 0.0, float(VOCAB - 1), ALU.max, ALU.min))
            nc.vector.tensor_copy(idu[:], c0).then_inc(ids_safe, 1)
            nc.vector.tensor_scalar(le, f, float(VOCAB - 1), None, ALU.is_le)
            then(nc.vector.tensor_scalar(ok, f, 0.0, None, ALU.is_ge))
            then(nc.vector.tensor_tensor(ok, ok, le, ALU.mult))
            dve.wait_ge(tok_in, 16)
            dve.wait_ge(consts_set, 1)

            def tok_logit(c):
                cols = slice(c % CHUNKS * TILES, (c % CHUNKS + 1) * TILES)
                dve.wait_ge(energy_done, c + 1)
                then(nc.vector.tensor_scalar(lg[:, 0, cols], ps[:, 3, cols], b2c, None, ALU.add))
                one = lg[:, 0, cols].rearrange("p (t o) -> p t o", o=1)
                then(nc.vector.tensor_reduce(lg[:, 1, cols], one, AX.X, ALU.max))
                nc.vector.tensor_tensor(lg[:, 2, cols], lg[:, 0, cols], lg[:, 1, cols], ALU.subtract).then_inc(logit_ready, 1)

            def tok_rows(c):
                cc = c % CHUNKS
                cols = slice(cc * TILES, (cc + 1) * TILES)
                dve.wait_ge(expw_done, c + 1)
                then(nc.vector.tensor_reduce(lg[:, 4, cols], lg[:, 3, cols].rearrange("p (t o) -> p t o", o=1), AX.X, ALU.add))
                then(nc.vector.reciprocal(lg[:, 4, cols], lg[:, 4, cols]))
                then(nc.vector.tensor_tensor(lg[:, 5, cols], lg[:, 3, cols], lg[:, 4, cols], ALU.mult))
                if cc == CHUNKS - 1:
                    then(nc.vector.memset(lg[TXT0:TXT0 + TXT, 5, G - 1:G], 1.0))
                for t in range(TILES):
                    g, r = cc * TILES + t, ROWS[t]
                    ins = nc.vector.tensor_scalar(xh[0:r, g, :], xh[0:r, g, :], lg[0:r, 5, g:g + 1], None, ALU.mult)
                ins.then_inc(h_ready, 1)
                dve.wait_ge(h_ready, c + 1)

            def statistics(src, c):
                for t in range(TILES):
                    g, r = c * TILES + t, ROWS[t]
                    ins = nc.vector.bn_stats(st[0:r, g, :], src[0:r, g, :])
                then(ins)
                nc.vector.memset(mv[ROWS[2]:P, c * TILES + 2, :], 1.0)
                for t in range(TILES):
                    g, r = c * TILES + t, ROWS[t]
                    ins = nc.vector.bn_aggr(mv[0:r, g, :], st[0:r, g, :])
                return ins

            def normalise(src, c, slot):
                for t in range(TILES):
                    g, r = c * TILES + t, ROWS[t]
                    ins = nc.vector.tensor_scalar(xln[0:r, slot, t, :], src[0:r, g, :], mv[0:r, g, 0:1], rs[0:r, g:g + 1],
                                                  ALU.subtract, ALU.mult)
                return ins

            def values(c):
                b, cc = divmod(c, CHUNKS)
                g, r = cc * TILES, ROWS[2]
                dve.wait_ge(v_done, c * TILES + 2)
                nc.vector.tensor_tensor(vs[b][:, g:g + 2, :], two_tiles(4), twice(bvr), ALU.add).then_inc(v_ready, 2)
                dve.wait_ge(v_done, (c + 1) * TILES)
                nc.vector.tensor_tensor(vs[b][0:r, g + 2, :], ps[0:r, 5, 0:D], bvr[0:r, :], ALU.add).then_inc(v_ready, 1)

            for c in range(NC):
                tok_logit(c)
                tok_rows(c)
                statistics(xh, c % CHUNKS).then_inc(var_ready, 1)
                if c == 0:
                    dve.wait_ge(txt_gathered, 16 * B)
                    for i in range(B):
                        nc.vector.tensor_scalar(txt[:, i, :], txt[:, i, :], ok[:, i:i + 1], None, ALU.mult).then_inc(txt_masked, 1)
                if c == 2:
                    dve.wait_ge(row_in, 16)
                if c >= 2:
                    values(c - 2)
                if c == 3:
                    dve.wait_ge(hi_split, 3)
                    nc.vector.scalar_tensor_tensor(out=orf[:, 1], in0=part(raw, RAW_COLS, "orf"), scalar=float(DK) ** -0.25,
                                                   in1=orf[:, 0].bitcast(F32), op0=ALU.mult, op1=ALU.subtract).then_inc(lo_split, 1)
                dve.wait_ge(rstd_ready, c + 1)
                if c >= 2:
                    dve.wait_ge(xlnT_turned, c - 1)
                normalise(xh, c % CHUNKS, c % 2).then_inc(xln_ready, 1)
            def split_x(b, c):
                if c == 0:
                    dve.wait_ge(xlnT_ready, 1)
                else:
                    dve.wait_ge(q_done, (b * CHUNKS + c) * KD)
                src = xlnT[:, bass.ds(b * CHUNKS + c, 1)].rearrange("p o k n -> p (o k n)")
                hi, lo = (xs[:, i].rearrange("p k n -> p (k n)") for i in range(2))
                then(nc.vector.tensor_scalar(hi, src, 1.0, None, ALU.mult))
                nc.vector.tensor_tensor(lo, src, hi.bitcast(F32), ALU.subtract).then_inc(xs_ready, 1)

            def keys(b, c, hh):
                dve.wait_ge(ksq_ready, (b * CHUNKS + c) * KD + hh + 1)
                nc.vector.scalar_tensor_tensor(out=ks[:, 1, hh, :], in0=ps[:, 2 + hh, 0:N], scalar=bkc[:, hh:hh + 1],
                                               in1=ks[:, 0, hh, :].bitcast(F32), op0=ALU.add, op1=ALU.subtract).then_inc(k_ready, 1)

            def queries(b, c, hh):
                dve.wait_ge(qsq_made, (b * CHUNKS + c) * KD + hh + 1)
                nc.vector.scalar_tensor_tensor(out=qs[:, 1, hh, :], in0=ps[:, 2 + hh, 0:N], scalar=bqc[:, hh:hh + 1],
                                               in1=qs[:, 0, hh, :].bitcast(F32), op0=ALU.add, op1=ALU.subtract).then_inc(q_ready, 1)
                then(nc.vector.tensor_copy(qsq[:, 0, hh, :], sq[:, hh, :]))
                nc.vector.tensor_tensor(qsq[:, 1, hh, :], sq[:, hh, :], qsq[:, 0, hh, :].bitcast(F32),
                                        ALU.subtract).then_inc(qsq_ready, 1)

            def norms(b, c):
                dve.wait_ge(kn_turned, b * CHUNKS + c + 1)
                turned = ps[:, 5, 0:TILES * P].rearrange("p (t k j) -> p t k j", t=TILES, j=BLK)
                nc.vector.tensor_copy(kn[:, 0:2], turned[:, 0:2, 0:KD, 0:HPH])
                nc.vector.tensor_copy(kn[0:ROWS[2], 2], turned[0:ROWS[2], 2, 0:KD, 0:HPH]).then_inc(kn_ready, 1)

            split_x(0, 0)
            values(NC - 2)
            keys(0, 0, 0)
            keys(0, 0, 1)
            values(NC - 1)
            queries(0, 0, 0)
            norms(0, 0)
            assert steps[0] == DVE_FIRST, steps[0]
            nc.vector.memset(kvr[:], 0.0).then_inc(fin_ready, 1)
            dve.wait_ge(rest_in, 16)

            with dve.Fori(0, B) as b:
                base[0] = DVE_FIRST + b * DVE_STEPS
                steps[0] = 0

                def exponents(c, t):
                    g, r = c * TILES + t, ROWS[t]
                    if t == 0:
                        dve.wait_ge(kn_ready, b * CHUNKS + c + 1)
                    for hh in range(KD):
                        dve.wait_ge(kproj_done, (b * G + g) * KD + hh + 1)
                        if g >= RING:
                            dve.wait_ge(kv_done, b * G + g - RING + 1)
                            dve.wait_ge(ksum_ready, b * G + g - RING + 1)
                        nrm = kn[0:r, t, hh, :].rearrange("p (i o) -> p i o", o=1)
                        nc.vector.tensor_tensor(kphi[0:r, g % RING, hh, :].rearrange("p (i m) -> p i m", m=M),
                                                ps[0:r, 4 + hh, :].rearrange("p (i m) -> p i m", m=M),
                                                nrm.to_broadcast([r, HPH, M]), ALU.subtract).then_inc(karg_ready, 1)

                for c in range(CHUNKS):
                    exponents(c, 0)
                    queries(b, c, 1)
                    if c + 1 < CHUNKS:
                        split_x(b, c + 1)
                    exponents(c, 1)
                    exponents(c, 2)
                    if c + 1 < CHUNKS:
                        keys(b, c + 1, 0)
                        keys(b, c + 1, 1)
                        norms(b, c + 1)
                        queries(b, c + 1, 0)
                dve.wait_ge(kvall_done, b + 1)
                for hh in range(KD):
                    nc.vector.tensor_tensor(kvm[:, hh, :], ps[:, 6 + hh, 0:P], mask, ALU.mult)
                    ins = nc.vector.scalar_tensor_tensor(out=kvm[:, KD + hh, :], in0=ps[:, 6 + hh, P:2 * P],
                                                         scalar=KERNEL_EPS * L, in1=mask, op0=ALU.add, op1=ALU.mult)
                ins.then_inc(kvm_ready, 1)
                dve.wait_ge(kvm_ready, b + 1)
                then(nc.vector.tensor_reduce(kvr[:, 0, :], kvm[:], AX.X, ALU.add))
                nc.vector.tensor_scalar(kvr[:, 1, :], kvr[:, 0, :], KERNEL_EPS, None, ALU.mult)
                dve.wait_ge(kvT_turned, b + 1)
                nc.vector.tensor_copy(kvs[:].rearrange("p a m -> p (a m)"), ps[:, 2, :]).then_inc(kvs_ready, 1)
                dve.wait_ge(kvs_ready, b + 1)

                def attend(c):
                    turned = rden[:].rearrange("p k n -> p (k n)")
                    dve.wait_ge(nd_ready, (b * CHUNKS + c + 1) * KD)
                    if c >= 1:
                        dve.wait_ge(att_ready, b * CHUNKS + c)
                    then(nc.vector.transpose(turned, den[c]))
                    then(nc.vector.reciprocal(rec[:], rden[:].rearrange("p k (n i d) -> p (k n) i d", i=2, d=DK)[:, :, :, 0]))
                    then(nc.vector.tensor_copy(den[c].rearrange("p (n d) -> p n d", d=DK),
                                               rec[:].rearrange("p n (i o) -> p (n i) o", o=1).to_broadcast([P, 2 * NB, DK])))
                    then(nc.vector.transpose(turned, den[c]))
                    nc.vector.tensor_tensor(att[:, c], att[:, c], rden[:], ALU.mult).then_inc(att_ready, 1)

                def residual(c):
                    g, r = c * TILES, ROWS[2]
                    dve.wait_ge(wo_done, b * G + g + 2)
                    if g == 0:
                        dve.wait_ge(out_stored, b * 16 * 2 * CHUNKS + 1)
                    nc.vector.tensor_tensor(h2[:, g:g + 2, :], two_tiles(WO_BANKS[c]), hb[:, bass.ds(b * G + g, 2), :], ALU.add).then_inc(h2_ready, 2)
                    dve.wait_ge(wo_done, b * G + g + 3)
                    hb_g = hb[0:r, bass.ds(b * G + g + 2, 1), :].rearrange("p o d -> p (o d)")
                    nc.vector.tensor_tensor(h2[0:r, g + 2, :], ps[0:r, WO_BANKS[c] + 1, 0:D], hb_g, ALU.add).then_inc(h2_ready, 1)
                    dve.wait_ge(h2_ready, b * G + (c + 1) * TILES)
                    statistics(h2, c).then_inc(var2_ready, 1)

                def normalise_h2(c):
                    dve.wait_ge(rstd2_ready, b * CHUNKS + c + 1)
                    if c >= 2:
                        dve.wait_ge(xln2T_turned, b * CHUNKS + c - 1)
                    normalise(h2, c, c % 2).then_inc(xln2_ready, 1)

                def low_rank(c):
                    dve.wait_ge(phi_ready, b * CHUNKS + c + 1)
                    up = slice(RANK, P)
                    nc.vector.tensor_tensor(pS[up, c % 2, :], ps[up, 2, 0:N], pS[up, c % 2, :].bitcast(F32),
                                            ALU.subtract).then_inc(p_ready, 1)

                def low_result(c):
                    dve.wait_ge(u_done, b * CHUNKS + c + 1)
                    nc.vector.tensor_copy(uT[:], ps[:, 1, 0:N]).then_inc(u_ready, 1)

                def result(c):
                    dve.wait_ge(h2b_ready, b * G + (c + 1) * TILES)
                    g, r = c * TILES, ROWS[2]
                    dve.wait_ge(y_done, b * G + g + 2)
                    nc.vector.tensor_tensor(h2[:, g:g + 2, :], two_tiles(0), h2[:, g:g + 2, :], ALU.add).then_inc(fin_ready, 2)
                    dve.wait_ge(y_done, b * G + g + 3)
                    nc.vector.tensor_tensor(h2[0:r, g + 2, :], ps[0:r, 1, 0:D], h2[0:r, g + 2, :], ALU.add).then_inc(fin_ready, 1)

                attend(0)
                attend(1)
                residual(0)
                attend(2)
                residual(1)
                low_rank(0)
                normalise_h2(1)
                residual(2)
                normalise_h2(2)
                low_rank(1)
                low_result(0)
                result(0)
                low_rank(2)
                low_result(1)
                result(1)
                split_x(b, CHUNKS)
                keys(b, CHUNKS, 0)
                keys(b, CHUNKS, 1)
                low_result(2)
                result(2)
                queries(b, CHUNKS, 0)
                norms(b, CHUNKS)
                assert steps[0] == DVE_STEPS, steps[0]

        @block.tensor
        def _(pe):
            def mm3(dst, a, b, cols_a, cols_b, start=True, stop=True):
                nc.tensor.matmul(dst, a(1, cols_a), b(0, cols_b), start=start, stop=False)
                nc.tensor.matmul(dst, a(0, cols_a), b(1, cols_b), start=False, stop=False)
                return nc.tensor.matmul(dst, a(0, cols_a), b(0, cols_b), start=False, stop=stop)

            def row_tile(t, bank):
                return ps[0:ROWS[t], bank + t // 2, t % 2 * D:(t % 2 + 1) * D]

            pe.wait_ge(tok_in, 16)
            pe.wait_ge(consts_set, 1)

            def turn_x(c):
                cc = c % CHUNKS
                pe.wait_ge(x_in[cc], 32 * (c // CHUNKS) + 32)
                if cc == CHUNKS - 1:
                    pe.wait_ge(txt_in, 16 * (c // CHUNKS) + 16)
                if c >= 1:
                    pe.wait_ge(xT_ready, c)
                for k in range(KD):
                    for t in range(TILES):
                        g, r = cc * TILES + t, ROWS[t]
                        ins = nc.tensor.transpose(ps[:, k, tile_cols(t)], xh[0:r, g, k * P:(k + 1) * P], idn[0:r, 0:r])
                ins.then_inc(xT_turned, 1)

            def turn_xln(c):
                pe.wait_ge(xln_ready, c + 1)
                if c >= 1:
                    pe.wait_ge(xlnT_ready, c)
                for k in range(KD):
                    for t in range(TILES):
                        r = ROWS[t]
                        ins = nc.tensor.transpose(ps[:, 6 + k, tile_cols(t)], xln[0:r, c % 2, t, k * P:(k + 1) * P], idn[0:r, 0:r])
                ins.then_inc(xlnT_turned, 1)

            def values(c):
                pe.wait_ge(xlnT_ready, c + 1)
                if c == 0:
                    pe.wait_ge(row_in, 16)
                if c >= 1:
                    pe.wait_ge(v_ready, c * TILES)
                for t in range(TILES):
                    r = ROWS[t]
                    for k in range(KD):
                        ins = nc.tensor.matmul(row_tile(t, 4), xlnT[:, c, k, tile_cols(t)], wv[:, k, :],
                                               start=k == 0, stop=k == KD - 1)
                    ins.then_inc(v_done, 1)

            turn_x(0)
            for c in range(NC):
                pe.wait_ge(xT_ready, c + 1)
                if c >= 1:
                    pe.wait_ge(tanh_done, c)
                for k in range(KD):
                    ins = nc.tensor.matmul(ps[:, 2, 0:N], w1[:, k, :], xT[:, c % 2, k, :], start=k == 0, stop=k == KD - 1)
                ins.then_inc(tok_done, 1)
                if c + 1 < NC:
                    turn_x(c + 1)
                pe.wait_ge(tanh_done, c + 1)
                if c >= 1:
                    pe.wait_ge(logit_ready, c)
                for t in range(TILES):
                    g = c % CHUNKS * TILES + t
                    ins = nc.tensor.matmul(ps[:, 3, g:g + 1], hT[:, c % 2, t * P:(t + 1) * P], w2, start=True, stop=True)
                ins.then_inc(energy_done, 1)
                if c >= 2:
                    values(c - 2)
                if c >= 1:
                    turn_xln(c - 1)
            def keys(b, c, hh):
                pe.wait_ge(xs_ready, b * CHUNKS + c + 1)
                if c >= 1:
                    pe.wait_ge(q_ready, (b * CHUNKS + c - 1) * KD + hh + 1)
                for k in range(KD):
                    ins = mm3(ps[:, 2 + hh, 0:N], lambda i, s: wk[:, i, k, s], lambda i, s: xs[:, i, k, s],
                              slice(hh * P, (hh + 1) * P), slice(0, N), k == 0, k == KD - 1)
                ins.then_inc(k_done, 1)

            def queries(b, c, hh):
                pe.wait_ge(k_ready, (b * CHUNKS + c) * KD + hh + 1)
                for k in range(KD):
                    ins = mm3(ps[:, 2 + hh, 0:N], lambda i, s: wq[:, i, k, s], lambda i, s: xs[:, i, k, s],
                              slice(hh * P, (hh + 1) * P), slice(0, N), k == 0, k == KD - 1)
                ins.then_inc(q_done, 1)

            def norms(b, c):
                pe.wait_ge(ksq_ready, (b * CHUNKS + c + 1) * KD)
                if c >= 1:
                    pe.wait_ge(karg_ready, (b * CHUNKS + c) * TILES * KD - 1)
                for hh in range(KD):
                    ins = nc.tensor.matmul(ps[hh * BLK:(hh + 1) * BLK, 4, 0:N], ncol, sq[:, hh, :], start=True, stop=True,
                                           tile_position=(0, hh * BLK))
                ins.then_inc(kn_done, 1)

            def turn_norms(b, c):
                pe.wait_ge(knT_ready, b * CHUNKS + c + 1)
                if c >= 1:
                    pe.wait_ge(karg_ready, (b * CHUNKS + c) * TILES * KD)
                for t in range(TILES):
                    ins = nc.tensor.transpose(ps[0:ROWS[t], 5, t * P:(t + 1) * P], knT[:, tile_cols(t)], idn)
                ins.then_inc(kn_turned, 1)

            values(NC - 2)
            pe.wait_ge(hi_split, 5)
            pe.wait_ge(lo_split, 4)
            pe.wait_ge(logit_ready, NC)
            keys(0, 0, 0)
            keys(0, 0, 1)
            turn_xln(NC - 1)
            values(NC - 1)
            pe.wait_ge(v_ready, NC * TILES)
            pe.wait_ge(rest_in, 16)
            norms(0, 0)
            queries(0, 0, 0)
            turn_norms(0, 0)
            queries(0, 0, 1)
            pe.wait_ge(vsum_ready, B * (G - 1))

            with pe.Fori(0, B) as b:
                def kproj(c, t):
                    g, r = c * TILES + t, ROWS[t]
                    if t == 0:
                        pe.wait_ge(k_ready, (b * CHUNKS + c + 1) * KD)
                    for hh in range(KD):
                        if t == 0:
                            pe.wait_ge(kn_ready, b * CHUNKS + c + 1)
                        else:
                            pe.wait_ge(karg_ready, (b * G + g - 1) * KD + hh + 1)
                        mm3(ps[0:r, 4 + hh, :], lambda i, s: ks[:, i, hh, s], lambda i, s: orf[:, i, s],
                            tile_cols(t), slice(0, HPH * M)).then_inc(kproj_done, 1)

                def qproj(c, p):
                    hh, j = divmod(p, PPH)
                    if p == 0:
                        pe.wait_ge(fin_ready, b * G + 1)
                    if c > 0 or p >= 2:
                        pe.wait_ge(qphi_ready, (b * CHUNKS + c) * PAIRS + p - 1)
                    pe.wait_ge(q_ready, (b * CHUNKS + c) * KD + hh + 1)
                    s = slice(j * P, (j + 1) * P)
                    mm3(ps[:, p % 2, 0:N], lambda i, s: orf[:, i, s], lambda i, s: qs[:, i, hh, s], s, slice(0, N), True, False)
                    pe.wait_ge(qsq_ready, (b * CHUNKS + c) * KD + hh + 1)
                    nc.tensor.matmul(ps[:, p % 2, 0:N], nblk[:, s], qsq[:, 1, hh, :], start=False, stop=False)
                    nc.tensor.matmul(ps[:, p % 2, 0:N], nblk[:, s], qsq[:, 0, hh, :], start=False, stop=True).then_inc(qproj_done, 1)

                def kv(c, t):
                    g, r = c * TILES + t, ROWS[t]
                    pe.wait_ge(kphi_ready, (b * G + g + 1) * KD)
                    for p in range(PAIRS):
                        hh, j = divmod(p, PPH)
                        ins = nc.tensor.matmul(ps[BLK * j:BLK * (j + 1), 6 + hh, 0:P], vs[0][0:r, g, BLK * p:BLK * (p + 1)],
                                               kphi[0:r, g % RING, hh, j * P:(j + 1) * P], start=g == 0, stop=False,
                                               tile_position=(0, BLK * j), skip_group_check=True)
                    ins.then_inc(kv_done, 1)

                def kv_sums():
                    pe.wait_ge(ksum_ready, (b + 1) * G)
                    for p in range(PAIRS):
                        hh, j = divmod(p, PPH)
                        nc.tensor.matmul(ps[BLK * j:BLK * (j + 1), 6 + hh, 0:P], vs[0][:, G, BLK * p:BLK * (p + 1)], epsm[:],
                                         start=False, stop=True, tile_position=(0, BLK * j), skip_group_check=True)
                    for p in range(PAIRS):
                        hh, j = divmod(p, PPH)
                        ins = nc.tensor.matmul(ps[BLK * j:BLK * (j + 1), 6 + hh, P:2 * P], ones[:], ksum[:, p * P:(p + 1) * P],
                                               start=False, stop=True, tile_position=(0, BLK * j), skip_group_check=True)
                    ins.then_inc(kvall_done, 1)

                def kv_turn():
                    pe.wait_ge(kvm_ready, b + 1)
                    pe.wait_ge(q_ready, (b + 1) * CHUNKS * KD)
                    for i in range(2 * KD):
                        ins = nc.tensor.transpose(ps[:, 2, i * P:(i + 1) * P], kvm[:, i, :], idn)
                    ins.then_inc(kvT_turned, 1)

                def numden(c, hh):
                    if c == 0 and hh == 0:
                        pe.wait_ge(kvs_ready, b + 1)
                    if c == CHUNKS - 1:
                        pe.wait_ge(qphi_ready, (b + 1) * CHUNKS * PAIRS)
                    if 2 * c + hh >= 3:
                        pe.wait_ge(nd_ready, b * CHUNKS * KD + 2 * c + hh - 2)
                    for s in range(2):
                        for j in range(PPH):
                            ins = nc.tensor.matmul(ps[BLK * j:BLK * (j + 1), ND_BANKS[c][hh] + s, 0:N],
                                                   kvs[:, s * KD + hh, BLK * j:BLK * (j + 1)],
                                                   work[:, c, hh * PPH + j, :], start=True, stop=True,
                                                   tile_position=(0, BLK * j))
                    ins.then_inc(nd_done, 1)

                def project(c, tiles=range(TILES)):
                    pe.wait_ge(att_ready, b * CHUNKS + c + 1)
                    if c == 0:
                        pe.wait_ge(qphi_ready, (b + 1) * CHUNKS * PAIRS)
                    elif c == 1:
                        pe.wait_ge(nd_ready, (b + 1) * CHUNKS * KD)
                    else:
                        pe.wait_ge(h2_ready, b * G + TILES)
                    for t in tiles:
                        for k in range(KD):
                            ins = nc.tensor.matmul(row_tile(t, WO_BANKS[c]), att[:, c, k, tile_cols(t)], wo[:, k, :],
                                                   start=k == 0, stop=k == KD - 1)
                        ins.then_inc(wo_done, 1)

                def turn_xln2(c):
                    pe.wait_ge(xln2_ready, b * CHUNKS + c + 1)
                    if c == 0:
                        pe.wait_ge(nd_ready, b * CHUNKS * KD + 4)
                    else:
                        pe.wait_ge(p_ready, b * CHUNKS + c)
                    for k in range(KD):
                        for t in range(TILES):
                            r = ROWS[t]
                            ins = nc.tensor.transpose(ps[:, 2 + k, tile_cols(t)], xln[0:r, c % 2, t, k * P:(k + 1) * P], idn[0:r, 0:r])
                    ins.then_inc(xln2T_turned, 1)

                def down_in(c):
                    pe.wait_ge(xln2T_ready, b * CHUNKS + c + 1)
                    for k in range(KD):
                        ins = nc.tensor.matmul(ps[:, 2, 0:N], u1[:, k, :], xln2T[:, k, :], start=k == 0, stop=k == KD - 1)
                    ins.then_inc(p_done, 1)

                def up(c, i):
                    if i == 0:
                        pe.wait_ge(p_ready, b * CHUNKS + c + 1)
                    if c == 0 and i < 4:
                        pe.wait_ge(h2_ready, b * G + 2 * TILES)
                    else:
                        pe.wait_ge(gelu_ready, (b * CHUNKS + c) * FT + i - 3)
                    f = FORDER[i]
                    nc.tensor.matmul(ps[:, 4 + i % 4, 0:N], v1[:, 1, f * P:(f + 1) * P], pS[:, c % 2, :], start=True, stop=False)
                    nc.tensor.matmul(ps[:, 4 + i % 4, 0:N], v1[:, 0, f * P:(f + 1) * P], pS[:, c % 2, :], start=False,
                                     stop=True).then_inc(ff_done, 1)

                def down(c, i):
                    if i == 0:
                        if c == 0:
                            pe.wait_ge(h2_ready, (b + 1) * G)
                        else:
                            pe.wait_ge(fin_ready, b * G + c * TILES + 1)
                    pe.wait_ge(gelu_ready, (b * CHUNKS + c) * FT + i + 1)
                    side = i % 2
                    ins = nc.tensor.matmul(ps[RANK * side:RANK * (side + 1), 1, 0:N], u2[:, FORDER[i], :], work[:, c, i, :],
                                           start=i < 2, stop=i >= FT - 2, tile_position=(0, RANK * side))
                    if i == FT - 1:
                        ins.then_inc(u_done, 1)

                def up_out(c):
                    pe.wait_ge(u_ready, b * CHUNKS + c + 1)
                    for t in range(TILES):
                        nc.tensor.matmul(row_tile(t, 0), uT[:, tile_cols(t)], v2, start=True, stop=True).then_inc(y_done, 1)

                for c in range(CHUNKS - 1):
                    kproj(c, 0)
                    qproj(c, 0)
                    kproj(c, 1)
                    qproj(c, 1)
                    kv(c, 0)
                    kproj(c, 2)
                    qproj(c, 2)
                    kv(c, 1)
                    qproj(c, 3)
                    keys(b, c + 1, 0)
                    kv(c, 2)
                    keys(b, c + 1, 1)
                    qproj(c, 4)
                    qproj(c, 5)
                    norms(b, c + 1)
                    qproj(c, 6)
                    turn_norms(b, c + 1)
                    queries(b, c + 1, 0)
                    qproj(c, 7)
                    queries(b, c + 1, 1)
                c = CHUNKS - 1
                kproj(c, 0)
                qproj(c, 0)
                kproj(c, 1)
                qproj(c, 1)
                kv(c, 0)
                kproj(c, 2)
                kv(c, 1)
                qproj(c, 2)
                kv(c, 2)
                qproj(c, 3)
                qproj(c, 4)
                kv_sums()
                qproj(c, 5)
                kv_turn()
                qproj(c, 6)
                numden(0, 0)
                numden(0, 1)
                qproj(c, 7)
                numden(1, 0)
                numden(1, 1)
                numden(2, 0)
                numden(2, 1)
                project(0)
                project(1)
                turn_xln2(0)
                project(2, [0])
                down_in(0)
                project(2, [1, 2])
                for c in range(CHUNKS):
                    for i in range(0 if c == 0 else 2, 4):
                        up(c, i)
                    if c + 1 < CHUNKS:
                        turn_xln2(c + 1)
                    down(c, 0)
                    down(c, 1)
                    up(c, 4)
                    up(c, 5)
                    if c + 1 < CHUNKS:
                        down_in(c + 1)
                    down(c, 2)
                    down(c, 3)
                    up(c, 6)
                    up(c, 7)
                    if c + 1 < CHUNKS:
                        for i in range(4, FT):
                            down(c, i)
                        up(c + 1, 0)
                        up(c + 1, 1)
                        up_out(c)
                keys(b, CHUNKS, 0)
                keys(b, CHUNKS, 1)
                for i in range(4, FT):
                    down(CHUNKS - 1, i)
                norms(b, CHUNKS)
                up_out(CHUNKS - 1)
                queries(b, CHUNKS, 0)
                turn_norms(b, CHUNKS)
                queries(b, CHUNKS, 1)
                pe.wait_ge(v_moved, 16 * (b + 1))


_OUT = ((2, 1056, 256), "float32")


def kernel(**inputs):
    import numpy as np
    import concourse.bacc as bacc
    from concourse.bass_utils import run_bass_kernel_spmd

    arg = {k.replace("L0_", ""): np.asarray(v) for k, v in inputs.items()}
    DK, M = 16, 64

    def tall(a):
        return a.reshape(-1, 128, a.shape[1]).transpose(1, 0, 2).reshape(128, -1)

    def same_rows(a):
        return np.broadcast_to(a[None, :], (128, a.shape[0]))

    def columns(a):
        return a.reshape(-1, 128).T

    orf = np.zeros((128, 8 * M), np.float32)
    for i in range(8):
        orf[DK * i:DK * (i + 1), M * i:M * (i + 1)] = arg["attn_orf"].T
    own = np.kron(np.eye(128 // DK), np.ones((DK, M)))
    cols = np.zeros((128, 32))
    cols[:, :8] = np.kron(np.eye(128 // DK), np.ones((DK, 1)))
    pair = np.kron(np.eye(2), np.ones((DK, M)))
    packed = {
        "ident": np.eye(128, dtype=np.float32),
        "W1": tall(arg["tok_W1"]), "b1": columns(arg["tok_b1"]), "W2": arg["tok_W2"],
        "b2": np.broadcast_to(arg["tok_b2"][None, :], (128, 1)),
        "WkT": tall(arg["attn_Wk"].T), "WqT": tall(arg["attn_Wq"].T), "WvT": tall(arg["attn_Wv"].T), "WoT": tall(arg["attn_Wo"].T),
        "bk": columns(arg["attn_bk"]), "bq": columns(arg["attn_bq"]), "bv": same_rows(arg["attn_bv"]), "bo": same_rows(arg["attn_bo"]),
        "orf": orf, "norm_block": (own * (-0.5 / DK ** 0.5)).astype(np.float32),
        "norm_cols": (cols * (0.5 / DK ** 0.5)).astype(np.float32),
        "head_mask": (np.tile(pair, (4, 1)) / M).astype(np.float32),
        "U1": tall(np.concatenate([arg["ffn_U1"], arg["ffn_U1"]], axis=1)),
        "V1": np.concatenate([arg["ffn_V1"], arg["ffn_V1"]], axis=0), "b1f": columns(arg["ffn_b1"]),
        "U2": tall(arg["ffn_U2"]), "V2": np.concatenate([arg["ffn_V2"], arg["ffn_V2"]], axis=0), "b2f": same_rows(arg["ffn_b2"]),
    }

    def pack(columns_of):
        return np.concatenate([packed[n] for n, _ in columns_of], axis=1)

    host = {"x": arg["x"], "ids": arg["x_txt"].T, "emb": arg["txt_w"], "tok_w": pack(TOK_COLS), "raw_w": pack(RAW_COLS),
            "row_w": pack(ROW_COLS), "rest_w": pack(REST_COLS)}
    nc = bacc.Bacc("TRN2", target_bir_lowering=False, num_devices=1)
    arrays, args = {}, []
    for name, a in host.items():
        a = np.ascontiguousarray(a)
        arrays[f"in_{name}"] = a
        args.append(nc.dram_tensor(f"in_{name}", a.shape, mybir.dt.from_np(a.dtype), kind="ExternalInput").ap())
    args.append(nc.dram_tensor("out_0", _OUT[0], mybir.dt.float32, kind="ExternalOutput").ap())
    build(nc, *args)
    r = run_bass_kernel_spmd(nc, [arrays], core_ids=[0])
    return r.results[0]["out_0"]
```

```python
from contextlib import ExitStack

import concourse.bass as bass
from concourse import mybir

ALU = mybir.AluOpType
ACT = mybir.ActivationFunctionType
AX = mybir.AxisListType
F32 = mybir.dt.float32
F32R = mybir.dt.float32r
I32 = mybir.dt.int32
U32 = mybir.dt.uint32

P = 128
CHUNKS = 3
TILES = 3
BLK = 32
KERNEL_EPS = 1e-6
NORM_EPS = 1e-5

TOK_COLS = [("ident", 128), ("W1", 256), ("b1", 1), ("W2", 1), ("b2", 1)]
RAW_COLS = [("WkT", 512), ("WqT", 512), ("orf_quad", 256), ("norm_quad", 256), ("V1", 1024)]
ROW_COLS = [("WvT", 512), ("bv", 256), ("bo", 256), ("bk", 2), ("bq", 2)]
REST_COLS = [("norm_cols", 32), ("head_mask", 128), ("WoT", 512), ("U1", 256), ("U2", 512), ("V2", 256), ("b1f", 8), ("b2f", 256)]


def width(columns):
    return sum(n for _, n in columns)


def build(nc, x, ids_in_dram, emb, tok_w, raw_w, row_w, rest_w, out):
    B, _, X, D = x.shape
    TXT = ids_in_dram.shape[0]
    VOCAB = emb.shape[0]
    L = X + TXT
    N = L // CHUNKS
    ROWS = [P, P, N - 2 * P]
    TXT0 = ROWS[2] - TXT
    G = CHUNKS * TILES
    NC = B * CHUNKS
    KD = D // P
    DK, M = 16, 64
    HPH = P // DK
    PAIRS = D // DK // 2
    PPH = PAIRS // KD
    RANK, FF = 64, 1024
    FT = FF // P
    FORDER = [f // 2 + FT // 2 * (f % 2) for f in range(FT)]
    RING = 3
    NB = KD * N // BLK
    assert KD * P == D and 2 * M == P and PPH * 2 * DK == P and N <= 512 and 2 * RANK == P and N % BLK == 0

    ctx = ExitStack()
    with ctx:
        def sb(name, shape, dt=F32):
            return ctx.enter_context(nc.sbuf_tensor(name, shape, dt))

        def sem(name):
            return ctx.enter_context(nc.semaphore(name))

        tokw = sb("tokw", [P, width(TOK_COLS)])
        roww = sb("roww", [P, width(ROW_COLS)])
        restw = sb("restw", [P, width(REST_COLS)])
        work = sb("work", [P, CHUNKS, PAIRS, N])
        flat = work[:].rearrange("p c a n -> p (c a n)")

        def part(tile, columns, name):
            at = 0
            for n, wide in columns:
                if n == name:
                    return tile[:, at:at + wide]
                at += wide

        def halves(ap, k=KD):
            return ap.rearrange("p (k n) -> p k n", k=k)

        idn = part(tokw, TOK_COLS, "ident")
        w1 = halves(part(tokw, TOK_COLS, "W1"))
        b1c, w2, b2c = (part(tokw, TOK_COLS, n) for n in ("b1", "W2", "b2"))
        wv = halves(part(roww, ROW_COLS, "WvT"))
        bvr, bor, bkc, bqc = (part(roww, ROW_COLS, n) for n in ("bv", "bo", "bk", "bq"))
        wo = halves(part(restw, REST_COLS, "WoT"))
        u1 = halves(part(restw, REST_COLS, "U1"))
        u2 = halves(part(restw, REST_COLS, "U2"), FT)
        v2, b1f, b2r, ncol, mask = (part(restw, REST_COLS, n) for n in ("V2", "b1f", "b2f", "norm_cols", "head_mask"))
        raw = flat[:, 0:width(RAW_COLS)]
        at = width(RAW_COLS)
        x0 = flat[:, at:at + G * D].rearrange("p (g d) -> p g d", d=D)
        at += G * D
        xT = flat[:, at:at + 2 * KD * N].rearrange("p (s k n) -> p s k n", s=2, k=KD)
        at += 2 * KD * N
        hT = flat[:, at:at + 2 * TILES * P].rearrange("p (s n) -> p s n", s=2)
        at += 2 * TILES * P
        assert at <= CHUNKS * PAIRS * N
        wk = sb("wk", [P, 2, KD, D], F32R)
        wq = sb("wq", [P, 2, KD, D], F32R)
        quad = sb("quad", [P, 3, 2 * P], F32R)
        v1 = sb("v1", [P, 2, FF], F32R)
        ones = sb("ones", [P, 2 * DK])
        epsm = sb("epsm", [P, P])
        mhalf = sb("mhalf", [P, TILES])
        neps = sb("neps", [P, TILES])
        ids = sb("ids", [TXT, B], I32)
        idf = sb("idf", [TXT, 4, B])
        idu = sb("idu", [TXT, B], U32)
        lg = sb("lg", [P, 6, G])
        hb = sb("hb", [P, B * G, D])
        xlnT = sb("xlnT", [P, NC, KD, N])
        vs = [sb("v_cur", [P, G + 1, D]), sb("v_next", [P, G + 1, D])]
        st = sb("st", [P, G, 6])
        mv = sb("mv", [P, G, 2])
        ve = sb("ve", [P, G])
        nm, nmr = sb("nm", [P, TILES]), sb("nmr", [P, TILES])
        zero = sb("zero", [P, TILES])
        rs = sb("rs", [P, G])
        xln = sb("xln", [P, 2, TILES, D])
        xs = sb("xs", [P, 2, KD, N], F32R)
        ks = sb("ks", [P, 2, KD, N], F32R)
        qs = sb("qs", [P, 2, KD, N], F32R)
        ksq = sb("ksq", [P, KD, N])
        sq = sb("sq", [P, KD, N])
        qsq = sb("qsq", [P, 2, KD, N], F32R)
        knT = sb("knT", [P, N])
        kn = sb("kn", [P, TILES, KD, HPH])
        kphi = sb("kphi", [P, RING, KD, HPH * M])
        kflat = kphi[:].rearrange("p g k m -> p (g k m)")
        xh = [x0, kflat[:, 0:G * D].rearrange("p (g d) -> p g d", d=D)]
        assert (G + B) * D <= RING * KD * HPH * M
        txt = kflat[0:TXT, G * D:(G + B) * D].rearrange("p (b d) -> p b d", b=B)
        ksum = sb("ksum", [P, KD * HPH * M])
        kvm = sb("kvm", [P, 2 * KD, P])
        kvr = sb("kvr", [P, 2, 2 * KD])
        kvs = sb("kvs", [P, 2 * KD, P])
        rden = sb("rden", [P, KD, N])
        rec = sb("rec", [P, NB, 2])
        att = sb("att", [P, CHUNKS, KD, N])
        h2 = sb("h2", [P, G, D])
        den = [kphi[:, c].rearrange("p k m -> p (k m)")[:, 0:KD * N] for c in range(CHUNKS)]
        xln2T = sb("xln2T", [P, KD, N])
        pS = sb("pS", [P, 2, N], F32R)
        uT = sb("uT", [P, N])

        ps = ctx.enter_context(nc.psum_tensor("ps", [P, 8, 512], F32))

        ids_loaded, tok_in, raw_in, row_in, rest_in = (sem(n) for n in ("ids_loaded", "tok_in", "raw_in", "row_in", "rest_in"))
        txt_in = [sem(f"txt_in{b}") for b in range(B)]
        x_in = [sem(f"x_in{c}") for c in range(NC)]
        consts_set, pads_set = sem("consts_set"), sem("pads_set")
        ids_safe, txt_gathered, txt_masked = sem("ids_safe"), sem("txt_gathered"), sem("txt_masked")
        hi_split, lo_split = sem("hi_split"), sem("lo_split")
        xT_turned, xT_ready = sem("xT_turned"), sem("xT_ready")
        tok_done, tanh_done, energy_done = sem("tok_done"), sem("tanh_done"), sem("energy_done")
        logit_ready, expw_done, h_ready = sem("logit_ready"), sem("expw_done"), sem("h_ready")
        var_ready, rstd_ready, xln_ready = sem("var_ready"), sem("rstd_ready"), sem("xln_ready")
        xlnT_turned, xlnT_ready = sem("xlnT_turned"), sem("xlnT_ready")
        v_done, v_ready, vsum_ready, hb_ready = sem("v_done"), sem("v_ready"), sem("vsum_ready"), sem("hb_ready")
        xs_ready = sem("xs_ready")
        k_done, ksq_ready, k_ready = sem("k_done"), sem("ksq_ready"), sem("k_ready")
        q_done, qsq_made, q_ready, qsq_ready = sem("q_done"), sem("qsq_made"), sem("q_ready"), sem("qsq_ready")
        kn_done, knT_ready, kn_turned, kn_ready = sem("kn_done"), sem("knT_ready"), sem("kn_turned"), sem("kn_ready")
        kproj_done, karg_ready, kphi_ready = sem("kproj_done"), sem("karg_ready"), sem("kphi_ready")
        qproj_done, qphi_ready = sem("qproj_done"), sem("qphi_ready")
        kv_done, ksum_ready, kvall_done, v_moved = sem("kv_done"), sem("ksum_ready"), sem("kvall_done"), sem("v_moved")
        kvm_ready, kvT_turned, kvs_ready = sem("kvm_ready"), sem("kvT_turned"), sem("kvs_ready")
        xs_hi_ready = sem("xs_hi_ready")
        nd_done, den_ready, nd_ready, att_ready = (sem(n) for n in ("nd_done", "den_ready", "nd_ready", "att_ready"))
        rden_ready = sem("rden_ready")
        wo_done, h2_ready, h2b_ready = sem("wo_done"), sem("h2_ready"), sem("h2b_ready")
        var2_ready, rstd2_ready, xln2_ready = sem("var2_ready"), sem("rstd2_ready"), sem("xln2_ready")
        xln2T_turned, xln2T_ready = sem("xln2T_turned"), sem("xln2T_ready")
        p_done, phi_ready, p_ready, ff_done, gelu_ready = (sem(n) for n in ("p_done", "phi_ready", "p_ready", "ff_done", "gelu_ready"))
        u_done, u_ready, y_done = sem("u_done"), sem("u_ready"), sem("y_done")
        fin_ready, out_stored = sem("fin_ready"), sem("out_stored")
        dve_step, pool_step = sem("dve_step"), sem("pool_step")

        ND_BANKS = [(2, 4), (6, 2), (4, 6)]

        KN_BANKS = [0, 4]

        WO_BANKS = [0, 4, 0]

        HALF = P // 2
        QUAD = [slice(0, HALF), slice(HALF, P)]

        def tile_cols(t):
            return slice(t * P, t * P + ROWS[t])

        block = ctx.enter_context(nc.Block())

        @block.sync
        def _(sp):
            def load_x(c):
                b, cc = divmod(c, CHUNKS)
                t0 = cc * N
                sp.dma_start(xh[b][:, cc * TILES:cc * TILES + 2, :],
                             x[b, 0, t0:t0 + 2 * P, :].rearrange("(t p) d -> p t d", p=P)).then_inc(x_in[c], 16)
                rows = ROWS[2] if cc < CHUNKS - 1 else TXT0
                sp.dma_start(xh[b][0:rows, cc * TILES + 2, :],
                             x[b, 0, t0 + 2 * P:t0 + 2 * P + rows, :]).then_inc(x_in[c], 16)
            load_x(0)
            load_x(1)
            load_x(2)

            def load_txt(b):
                sp.dma_start(xh[b][TXT0:TXT0 + TXT, G - 1, :], txt[:, b, :]).then_inc(txt_in[b], 16)

            load_x(CHUNKS)
            sp.wait_ge(txt_masked, B)
            load_txt(0)
            sp.dma_start(raw, raw_w).then_inc(raw_in, 16)
            for c in range(CHUNKS + 1, NC):
                load_x(c)
            load_txt(1)

            with sp.Fori(0, B) as b:
                sp.wait_ge(kvall_done, b + 1)
                sp.dma_start(vs[0][:], vs[1][:]).then_inc(v_moved, 16)
                for c in range(CHUNKS):
                    t0 = c * N
                    sp.wait_ge(fin_ready, b * G + c * TILES + 2 + 1)
                    sp.dma_start(out[b, t0:t0 + 2 * P, :].rearrange("(t p) d -> p t d", p=P),
                                 h2[:, c * TILES:c * TILES + 2, :]).then_inc(out_stored, 16)
                    sp.wait_ge(fin_ready, b * G + (c + 1) * TILES + 1)
                    sp.dma_start(out[b, t0 + 2 * P:t0 + N, :], h2[0:ROWS[2], c * TILES + 2, :]).then_inc(out_stored, 16)
            sp.wait_ge(out_stored, B * 16 * 2 * CHUNKS + 1)
            sp.wait_ge(v_moved, B * 16)

        @block.gpsimd
        def _(pool):
            nc.gpsimd.memset(neps[:], NORM_EPS)
            nc.gpsimd.memset(mhalf[:], -0.5)
            nc.gpsimd.memset(zero[:], 0.0)
            nc.gpsimd.memset(mv[:], 1.0)
            nc.gpsimd.memset(hT, 0.0).then_inc(consts_set, 1)
            pool.wait_ge(ids_safe, 1)
            for i in range(B):
                nc.gpsimd.indirect_dma_start(
                    out=txt[:, i, :], out_offset=None, in_=emb,
                    in_offset=bass.IndirectOffsetOnAxis(ap=idu[:, i:i + 1], axis=0)).then_inc(txt_gathered, 16)
            nc.gpsimd.memset(ones[:], 1.0)
            nc.gpsimd.memset(knT[:], 0.0)
            nc.gpsimd.memset(epsm[:], KERNEL_EPS)
            for i in range(B):
                nc.gpsimd.memset(vs[i][:, G, :], 0.0)
                nc.gpsimd.memset(vs[i][:, 2:G:TILES, :], 0.0).then_inc(pads_set, 1)
            nc.gpsimd.memset(rec[:], 1.0).then_inc(out_stored, 1)
            steps = [0]

            def sum_v(c):
                b, cc = divmod(c, CHUNKS)
                for t in range(TILES):
                    g = cc * TILES + t
                    pool.wait_ge(v_ready, c * TILES + t + 1)
                    if g >= 1:
                        r = ROWS[t]
                        a = vs[b][0:r, 0, :] if g == 1 else vs[b][0:r, G, :]
                        if g >= 2:
                            pool.wait_ge(vsum_ready, b * (G - 1) + g - 1)
                        nc.gpsimd.tensor_tensor(vs[b][0:r, G, :], a, vs[b][0:r, g, :], ALU.add).then_inc(vsum_ready, 1)

            def split_lo(dst, src, hi, n):
                pool.wait_ge(hi_split, n)
                nc.gpsimd.tensor_tensor(dst, src, hi.bitcast(F32), ALU.subtract).then_inc(lo_split, 1)

            for c in range(NC):
                cols = slice(c % CHUNKS * TILES, (c % CHUNKS + 1) * TILES)
                pool.wait_ge(var_ready, c + 1)
                nc.gpsimd.tensor_tensor(ve[:, cols], mv[:, cols, 1], neps[:], ALU.add).then_inc(pool_step, 1)
                steps[0] += 1
                pool.wait_ge(pool_step, steps[0])
                nc.gpsimd.tensor_tensor(rs[:, cols], ve[:, cols], mhalf[:], ALU.pow).then_inc(rstd_ready, 1)
                if c == 0:
                    pool.wait_ge(row_in, 16)
                for t in range(TILES):
                    g, r = c % CHUNKS * TILES + t, ROWS[t]
                    nc.gpsimd.tensor_tensor(hb[0:r, c * TILES + t, :], xh[c // CHUNKS][0:r, g, :], bor[0:r, :], ALU.add).then_inc(hb_ready, 1)
                if c == 1:
                    split_lo(wk[:, 1], halves(part(raw, RAW_COLS, "WkT")), wk[:, 0], 1)
                if c == 2:
                    split_lo(wq[:, 1], halves(part(raw, RAW_COLS, "WqT")), wq[:, 0], 2)
                if c == 3:
                    split_lo(v1[:, 1], part(raw, RAW_COLS, "V1"), v1[:, 0], 4)
                if c >= 2:
                    sum_v(c - 2)
            sum_v(NC - 2)
            sum_v(NC - 1)
            pool.wait_ge(vsum_ready, B * (G - 1))
            FIRST = steps[0]

            with pool.Fori(0, B) as b:
                for g in range(1, G - 1):
                    r = ROWS[g % TILES]
                    if g == 1 or g == TILES:
                        c = g // TILES + 1
                        hi, lo = (xs[:, i].rearrange("p k n -> p (k n)") for i in range(2))
                        src = xlnT[:, bass.ds(b * CHUNKS + c, 1)].rearrange("p o k n -> p (o k n)")
                        pool.wait_ge(xs_hi_ready, b * (CHUNKS - 1) + c)
                        nc.gpsimd.tensor_tensor(lo, src, hi.bitcast(F32), ALU.subtract).then_inc(xs_ready, 1)
                    pool.wait_ge(kphi_ready, b * KD * G + KD * (g + 1))
                    if g == 1:
                        nc.gpsimd.tensor_tensor(ksum[:], kphi[:, 0].rearrange("p k m -> p (k m)"),
                                                kphi[:, 1].rearrange("p k m -> p (k m)"), ALU.add).then_inc(ksum_ready, 2)
                    else:
                        pool.wait_ge(ksum_ready, b * (G - 1) + g)
                        nc.gpsimd.tensor_tensor(ksum[0:r, :], ksum[0:r, :], kphi[0:r, g % RING].rearrange("p k m -> p (k m)"),
                                                ALU.add).then_inc(ksum_ready, 1)
                steps[0] = 0

                def rstd2(c):
                    cols = slice(c * TILES, (c + 1) * TILES)
                    pool.wait_ge(var2_ready, b * CHUNKS + c + 1)
                    nc.gpsimd.tensor_tensor(ve[:, cols], mv[:, cols, 1], neps[:], ALU.add).then_inc(pool_step, 1)
                    steps[0] += 1
                    if c == 0:
                        nc.gpsimd.tensor_tensor(nm[:], zero[:], mv[:, cols, 0], ALU.subtract).then_inc(pool_step, 1)
                        steps[0] += 1
                    pool.wait_ge(pool_step, FIRST + b * (CHUNKS + 2) + steps[0])
                    power = nc.gpsimd.tensor_tensor(rs[:, cols], ve[:, cols], mhalf[:], ALU.pow)
                    if c == 0:
                        power.then_inc(pool_step, 1)
                        steps[0] += 1
                        pool.wait_ge(pool_step, FIRST + b * (CHUNKS + 2) + steps[0])
                        power = nc.gpsimd.tensor_tensor(nmr[:], nm[:], rs[:, cols], ALU.mult)
                    power.then_inc(rstd2_ready, 1)

                def add_b2(c):
                    pool.wait_ge(xln2_ready, b * CHUNKS + c + 1)
                    for t in range(TILES):
                        g, r = c * TILES + t, ROWS[t]
                        nc.gpsimd.tensor_tensor(h2[0:r, g, :], h2[0:r, g, :], b2r[0:r, :], ALU.add).then_inc(h2b_ready, 1)

                pool.wait_ge(rden_ready, b + 1)
                pool.wait_ge(nd_ready, (b * CHUNKS + 2) * KD)
                nc.gpsimd.tensor_tensor(att[:, 1], att[:, 1], rden[:], ALU.mult).then_inc(att_ready, 1)
                for c in range(CHUNKS):
                    rstd2(c)
                for c in range(CHUNKS):
                    add_b2(c)

        @block.scalar
        def _(act):
            act.dma_start(tokw[:], tok_w).then_inc(tok_in, 16)
            act.dma_start(ids[:], ids_in_dram).then_inc(ids_loaded, 16)
            act.wait_ge(consts_set, 1)
            nc.scalar.activation(lg[:, 3, :], neps[:, 0:1].to_broadcast([P, G]), ACT.Exp)
            act.wait_ge(tok_in, 16)

            def split_hi(c):
                if c == 1:
                    act.wait_ge(raw_in, 16)
                    nc.scalar.activation(wk[:, 0], halves(part(raw, RAW_COLS, "WkT")), ACT.Copy).then_inc(hi_split, 1)
                if c == 2:
                    nc.scalar.activation(wq[:, 0], halves(part(raw, RAW_COLS, "WqT")), ACT.Copy).then_inc(hi_split, 1)
                if c == 3:
                    nc.scalar.activation(quad[:, 2], part(raw, RAW_COLS, "norm_quad"), ACT.Copy)
                    nc.scalar.activation(quad[:, 0], part(raw, RAW_COLS, "orf_quad"), ACT.Copy, scale=float(DK) ** -0.25).then_inc(hi_split, 1)
                    nc.scalar.activation(v1[:, 0], part(raw, RAW_COLS, "V1"), ACT.Copy).then_inc(hi_split, 1)

            def turn_x(c):
                act.wait_ge(xT_turned, c + 1)
                if c >= 2:
                    act.wait_ge(tok_done, c - 1)
                nc.scalar.activation(xT[:, c % 2], ps[:, 0:KD, 0:N], ACT.Copy).then_inc(xT_ready, 1)

            def turn_xln(c):
                act.wait_ge(xlnT_turned, c + 1)
                nc.scalar.activation(xlnT[:, c], ps[:, 6:8, 0:N], ACT.Copy).then_inc(xlnT_ready, 1)

            turn_x(0)
            for c in range(NC):
                act.wait_ge(tok_done, c + 1)
                if c >= 2:
                    act.wait_ge(energy_done, c - 1)
                nc.scalar.activation(hT[:, c % 2, 0:N], ps[:, 2, 0:N], ACT.Tanh, bias=b1c).then_inc(tanh_done, 1)
                if c == 0:
                    act.dma_start(roww[:], row_w).then_inc(row_in, 16)
                if c == 2:
                    act.dma_start(restw[:], rest_w).then_inc(rest_in, 16)
                if c + 1 < NC:
                    turn_x(c + 1)
                if c == 2:
                    turn_xln(0)
                act.wait_ge(logit_ready, c + 1)
                cols = slice(c % CHUNKS * TILES, (c % CHUNKS + 1) * TILES)
                nc.scalar.activation(lg[:, 3, cols], lg[:, 2, cols], ACT.Exp).then_inc(expw_done, 1)
                split_hi(c)
                if c >= 2:
                    turn_xln(c - 1)
            def keys(b, c, hh):
                act.wait_ge(k_done, (b * CHUNKS + c) * KD + hh + 1)
                if c >= 1:
                    act.wait_ge(kproj_done, (b * CHUNKS + c) * TILES * KD)
                for u, rows in enumerate(QUAD):
                    nc.scalar.activation(ks[rows, u, hh, :], ps[rows, 2 + hh, 0:N], ACT.Identity, bias=bkc[rows, hh:hh + 1])
                nc.scalar.activation(ksq[:, hh, :], ps[:, 2 + hh, 0:N], ACT.Square, bias=bkc[:, hh:hh + 1]).then_inc(ksq_ready, 1)

            def queries(b, c, hh):
                act.wait_ge(q_done, (b * CHUNKS + c) * KD + hh + 1)
                if c >= 1:
                    act.wait_ge(qproj_done, (b * CHUNKS + c - 1) * PAIRS + (hh + 1) * PPH)
                if c >= 1:
                    act.wait_ge(qsq_ready, (b * CHUNKS + c - 1) * KD + hh + 1)
                for u, rows in enumerate(QUAD):
                    nc.scalar.activation(qs[rows, u, hh, :], ps[rows, 2 + hh, 0:N], ACT.Identity, bias=bqc[rows, hh:hh + 1])
                nc.scalar.activation(sq[:, hh, :], ps[:, 2 + hh, 0:N], ACT.Square, bias=bqc[:, hh:hh + 1]).then_inc(qsq_made, 1)

            def norms(b, c, bank=KN_BANKS[1]):
                act.wait_ge(kn_done, b * CHUNKS + c + 1)
                nc.scalar.activation(knT[0:KD * BLK, :], ps[0:KD * BLK, bank, 0:N], ACT.Copy).then_inc(knT_ready, 1)

            keys(0, 0, 0)
            keys(0, 0, 1)
            act.wait_ge(pads_set, B)
            norms(0, 0, KN_BANKS[0])
            turn_xln(NC - 1)
            queries(0, 0, 0)
            queries(0, 0, 1)
            act.wait_ge(rest_in, 16)

            def batch_entry(b, more):
                def exp_k(c, t):
                    g = c * TILES + t
                    for hh in range(KD):
                        act.wait_ge(karg_ready, (b * G + g) * KD + hh + 1)
                        nc.scalar.activation(kphi[0:ROWS[t], g % RING, hh, :], kphi[0:ROWS[t], g % RING, hh, :],
                                             ACT.Exp).then_inc(kphi_ready, 1)

                def exp_q(c, p):
                    act.wait_ge(qproj_done, (b * CHUNKS + c) * PAIRS + p + 1)
                    nc.scalar.activation(work[:, c, p, :], ps[:, p % 2, 0:N], ACT.Exp).then_inc(qphi_ready, 1)

                def normaliser(c, hh):
                    act.wait_ge(nd_done, (b * CHUNKS + c) * KD + hh + 1)
                    bank = ND_BANKS[c][hh]
                    nc.scalar.activation(den[c][:, hh * N:(hh + 1) * N], ps[:, bank + 1, 0:N], ACT.Identity,
                                         bias=kvr[:, 1, KD + hh:KD + hh + 1]).then_inc(den_ready, 1)
                    nc.scalar.activation(att[:, c, hh, :], ps[:, bank, 0:N], ACT.Identity,
                                         bias=kvr[:, 1, hh:hh + 1]).then_inc(nd_ready, 1)

                def normalise_first():
                    act.wait_ge(rstd2_ready, b * CHUNKS + 1)
                    for t in range(TILES):
                        ins = nc.scalar.activation(xln[0:ROWS[t], 0, t, :], h2[0:ROWS[t], t, :], ACT.Identity,
                                                   scale=rs[0:ROWS[t], t:t + 1], bias=nmr[0:ROWS[t], t:t + 1])
                    ins.then_inc(xln2_ready, 1)

                def turn_xln2(c):
                    act.wait_ge(xln2T_turned, b * CHUNKS + c + 1)
                    nc.scalar.activation(xln2T[:], ps[:, 2:4, 0:N], ACT.Copy).then_inc(xln2T_ready, 1)

                def low_rank(c):
                    act.wait_ge(p_done, b * CHUNKS + c + 1)
                    nc.scalar.activation(pS[:, c % 2, :], ps[:, 2, 0:N], ACT.Copy).then_inc(phi_ready, 1)

                def gelu(c, i):
                    act.wait_ge(ff_done, (b * CHUNKS + c) * FT + i + 1)
                    nc.scalar.activation(work[:, c, i, :], ps[:, 4 + i % 4, 0:N], ACT.Gelu_apprx_tanh,
                                         bias=b1f[:, FORDER[i]:FORDER[i] + 1]).then_inc(gelu_ready, 1)

                for c in range(CHUNKS - 1):
                    exp_q(c, 0)
                    exp_k(c, 0)
                    exp_q(c, 1)
                    exp_k(c, 1)
                    exp_q(c, 2)
                    exp_q(c, 3)
                    exp_k(c, 2)
                    keys(b, c + 1, 0)
                    keys(b, c + 1, 1)
                    exp_q(c, 4)
                    exp_q(c, 5)
                    queries(b, c + 1, 0)
                    norms(b, c + 1)
                    exp_q(c, 6)
                    exp_q(c, 7)
                    queries(b, c + 1, 1)
                c = CHUNKS - 1
                exp_k(c, 0)
                exp_q(c, 0)
                exp_q(c, 1)
                exp_k(c, 1)
                exp_q(c, 2)
                exp_q(c, 3)
                exp_k(c, 2)
                for p in range(4, PAIRS):
                    exp_q(c, p)
                act.wait_ge(kvs_ready, b + 1)
                normaliser(0, 0)
                normaliser(0, 1)
                normaliser(1, 0)
                normaliser(1, 1)
                normaliser(2, 0)
                normaliser(2, 1)
                nc.scalar.activation(lg[:, 3, :], neps[:, 0:1].to_broadcast([P, G]), ACT.Gelu_apprx_tanh)
                normalise_first()
                turn_xln2(0)
                low_rank(0)
                for c in range(CHUNKS):
                    for i in range(4):
                        gelu(c, i)
                    if c + 1 < CHUNKS:
                        turn_xln2(c + 1)
                    gelu(c, 4)
                    gelu(c, 5)
                    if c + 1 < CHUNKS:
                        low_rank(c + 1)
                    gelu(c, 6)
                    gelu(c, 7)
                if more:
                    keys(b, CHUNKS, 0)
                    keys(b, CHUNKS, 1)
                    norms(b, CHUNKS)
                    queries(b, CHUNKS, 0)
                    nc.scalar.activation(lg[:, 3, :], neps[:, 0:1].to_broadcast([P, G]), ACT.Exp)
                    queries(b, CHUNKS, 1)

            with act.Fori(0, B - 1) as b:
                batch_entry(b, True)
            batch_entry(B - 1, False)

        DVE_FIRST, DVE_STEPS = 45, 39

        @block.vector
        def _(dve):
            steps, base = [0], [0]

            def then(ins):
                ins.then_inc(dve_step, 1)
                steps[0] += 1
                dve.wait_ge(dve_step, base[0] + steps[0])

            def first(ins):
                ins.then_inc(dve_step, 1)
                steps[0] += 1

            def after_first():
                dve.wait_ge(dve_step, base[0] + steps[0])

            def two_tiles(bank):
                return ps[:, bank, :].rearrange("p (t d) -> p t d", t=2)

            def twice(row):
                return row.rearrange("p (o d) -> p o d", o=1).to_broadcast([P, 2, D])

            f, c0, ok, le = (idf[:, i, :] for i in range(4))
            dve.wait_ge(ids_loaded, 16)
            then(nc.vector.tensor_copy(f, ids[:]))
            then(nc.vector.tensor_scalar(c0, f, 0.0, float(VOCAB - 1), ALU.max, ALU.min))
            nc.vector.tensor_copy(idu[:], c0).then_inc(ids_safe, 1)
            nc.vector.tensor_scalar(le, f, float(VOCAB - 1), None, ALU.is_le)
            then(nc.vector.tensor_scalar(ok, f, 0.0, None, ALU.is_ge))
            then(nc.vector.tensor_tensor(ok, ok, le, ALU.mult))
            dve.wait_ge(txt_gathered, 16 * B)
            for i in range(B):
                nc.vector.tensor_scalar(txt[:, i, :], txt[:, i, :], ok[:, i:i + 1], None, ALU.mult).then_inc(txt_masked, 1)
            dve.wait_ge(tok_in, 16)
            dve.wait_ge(consts_set, 1)

            def token_weights(c):
                cc, xc = c % CHUNKS, xh[c // CHUNKS]
                cols = slice(cc * TILES, (cc + 1) * TILES)
                if c >= 1:
                    dve.wait_ge(rstd_ready, c)
                if c >= 3:
                    dve.wait_ge(xlnT_turned, c - 2)

                def between(t):
                    return normalise_tile(xh[(c - 1) // CHUNKS], (c - 1) % CHUNKS, (c - 1) % 2, t) if c >= 1 else None

                dve.wait_ge(energy_done, c + 1)
                first(nc.vector.tensor_scalar(lg[:, 0, cols], ps[:, 3, cols], b2c, None, ALU.add))
                between(0)
                after_first()
                one = lg[:, 0, cols].rearrange("p (t o) -> p t o", o=1)
                first(nc.vector.tensor_reduce(lg[:, 1, cols], one, AX.X, ALU.max))
                between(1)
                after_first()
                nc.vector.tensor_tensor(lg[:, 2, cols], lg[:, 0, cols], lg[:, 1, cols], ALU.subtract).then_inc(logit_ready, 1)
                last = between(2)
                if c >= 1:
                    last.then_inc(xln_ready, 1)
                dve.wait_ge(expw_done, c + 1)
                then(nc.vector.tensor_reduce(lg[:, 4, cols], lg[:, 3, cols].rearrange("p (t o) -> p t o", o=1), AX.X, ALU.add))
                then(nc.vector.reciprocal(lg[:, 4, cols], lg[:, 4, cols]))
                then(nc.vector.tensor_tensor(lg[:, 5, cols], lg[:, 3, cols], lg[:, 4, cols], ALU.mult))
                if cc == CHUNKS - 1:
                    then(nc.vector.memset(lg[TXT0:TXT0 + TXT, 5, G - 1:G], 1.0))
                for t in range(TILES):
                    g, r = cc * TILES + t, ROWS[t]
                    ins = nc.vector.tensor_scalar(xc[0:r, g, :], xc[0:r, g, :], lg[0:r, 5, g:g + 1], None, ALU.mult)
                ins.then_inc(h_ready, 1)
                dve.wait_ge(h_ready, c + 1)

            def statistics(src, c):
                for t in range(TILES):
                    g, r = c * TILES + t, ROWS[t]
                    ins = nc.vector.bn_stats(st[0:r, g, :], src[0:r, g, :])
                then(ins)
                nc.vector.memset(mv[ROWS[2]:P, c * TILES + 2, :], 1.0)
                for t in range(TILES):
                    g, r = c * TILES + t, ROWS[t]
                    ins = nc.vector.bn_aggr(mv[0:r, g, :], st[0:r, g, :])
                return ins

            def normalise_tile(src, c, slot, t):
                g, r = c * TILES + t, ROWS[t]
                return nc.vector.tensor_scalar(xln[0:r, slot, t, :], src[0:r, g, :], mv[0:r, g, 0:1], rs[0:r, g:g + 1],
                                               ALU.subtract, ALU.mult)

            def normalise(src, c, slot):
                for t in range(TILES):
                    ins = normalise_tile(src, c, slot, t)
                return ins

            def values(c):
                b, cc = divmod(c, CHUNKS)
                g, r = cc * TILES, ROWS[2]
                dve.wait_ge(v_done, c * TILES + 2)
                nc.vector.tensor_tensor(vs[b][:, g:g + 2, :], two_tiles(4), twice(bvr), ALU.add).then_inc(v_ready, 2)
                dve.wait_ge(v_done, (c + 1) * TILES)
                nc.vector.tensor_tensor(vs[b][0:r, g + 2, :], ps[0:r, 5, 0:D], bvr[0:r, :], ALU.add).then_inc(v_ready, 1)

            def split_x(b, c):
                if c == 0:
                    dve.wait_ge(xlnT_ready, 1)
                else:
                    dve.wait_ge(q_done, (b * CHUNKS + c) * KD)
                src = xlnT[:, bass.ds(b * CHUNKS + c, 1)].rearrange("p o k n -> p (o k n)")
                hi, lo = (xs[:, i].rearrange("p k n -> p (k n)") for i in range(2))
                if c % CHUNKS:
                    nc.vector.tensor_scalar(hi, src, 1.0, None, ALU.mult).then_inc(xs_hi_ready, 1)
                else:
                    then(nc.vector.tensor_scalar(hi, src, 1.0, None, ALU.mult))
                    nc.vector.tensor_tensor(lo, src, hi.bitcast(F32), ALU.subtract).then_inc(xs_ready, 1)

            for c in range(NC):
                token_weights(c)
                if c == NC - 1:
                    values(c - 2)
                statistics(xh[c // CHUNKS], c % CHUNKS).then_inc(var_ready, 1)
                if c == 2:
                    dve.wait_ge(row_in, 16)
                    dve.wait_ge(pads_set, B)
                if 2 <= c < NC - 1:
                    values(c - 2)
                if c == NC - 2:
                    dve.wait_ge(hi_split, 3)
                    nc.vector.scalar_tensor_tensor(out=quad[:, 1], in0=part(raw, RAW_COLS, "orf_quad"), scalar=float(DK) ** -0.25,
                                                   in1=quad[:, 0].bitcast(F32), op0=ALU.mult, op1=ALU.subtract).then_inc(lo_split, 1)
                    split_x(0, 0)

            def keys(b, c, hh):
                dve.wait_ge(ksq_ready, (b * CHUNKS + c) * KD + hh + 1)
                for u, rows in enumerate(QUAD):
                    ins = nc.vector.scalar_tensor_tensor(out=ks[QUAD[1 - u], u, hh, :], in0=ps[rows, 2 + hh, 0:N],
                                                         scalar=bkc[rows, hh:hh + 1], in1=ks[rows, u, hh, :].bitcast(F32),
                                                         op0=ALU.add, op1=ALU.subtract)
                ins.then_inc(k_ready, 1)

            def queries(b, c, hh):
                dve.wait_ge(qsq_made, (b * CHUNKS + c) * KD + hh + 1)
                for u, rows in enumerate(QUAD):
                    ins = nc.vector.scalar_tensor_tensor(out=qs[QUAD[1 - u], u, hh, :], in0=ps[rows, 2 + hh, 0:N],
                                                         scalar=bqc[rows, hh:hh + 1], in1=qs[rows, u, hh, :].bitcast(F32),
                                                         op0=ALU.add, op1=ALU.subtract)
                ins.then_inc(q_ready, 1)

            def squares(b, c, hh):
                dve.wait_ge(qsq_made, (b * CHUNKS + c) * KD + hh + 1)
                first(nc.vector.tensor_copy(qsq[QUAD[0], 0, hh, :], sq[QUAD[0], hh, :]))
                then(nc.vector.tensor_copy(qsq[QUAD[1], 1, hh, :], sq[QUAD[1], hh, :]))
                for u, rows in enumerate(QUAD):
                    ins = nc.vector.tensor_tensor(qsq[QUAD[1 - u], u, hh, :], sq[rows, hh, :], qsq[rows, u, hh, :].bitcast(F32),
                                                  ALU.subtract)
                ins.then_inc(qsq_ready, 1)

            def norms(b, c, bank=KN_BANKS[1]):
                dve.wait_ge(kn_turned, b * CHUNKS + c + 1)
                turned = ps[:, bank + 1, 0:TILES * P].rearrange("p (t k j) -> p t k j", t=TILES, j=BLK)
                nc.vector.tensor_copy(kn[:, 0:2], turned[:, 0:2, 0:KD, 0:HPH])
                nc.vector.tensor_copy(kn[0:ROWS[2], 2], turned[0:ROWS[2], 2, 0:KD, 0:HPH]).then_inc(kn_ready, 1)

            keys(0, 0, 0)
            dve.wait_ge(rstd_ready, NC)
            dve.wait_ge(xlnT_turned, NC - 2)
            normalise(xh[B - 1], CHUNKS - 1, (NC - 1) % 2).then_inc(xln_ready, 1)
            keys(0, 0, 1)
            values(NC - 2)
            norms(0, 0, KN_BANKS[0])
            queries(0, 0, 0)
            values(NC - 1)
            squares(0, 0, 0)
            assert steps[0] == DVE_FIRST, steps[0]
            nc.vector.memset(kvr[:], 0.0).then_inc(fin_ready, 1)
            dve.wait_ge(hb_ready, NC * TILES)
            dve.wait_ge(rest_in, 16)

            def batch_entry(b, more):
                base[0] = DVE_FIRST + b * DVE_STEPS
                steps[0] = 0

                def exponents(c, t):
                    g, r = c * TILES + t, ROWS[t]
                    if t == 0:
                        dve.wait_ge(kn_ready, b * CHUNKS + c + 1)
                    for hh in range(KD):
                        dve.wait_ge(kproj_done, (b * G + g) * KD + hh + 1)
                        if g >= RING:
                            dve.wait_ge(kv_done, b * G + g - RING + 1)
                            dve.wait_ge(ksum_ready, b * (G - 1) + g - RING + 1)
                        nrm = kn[0:r, t, hh, :].rearrange("p (i o) -> p i o", o=1)
                        nc.vector.tensor_tensor(kphi[0:r, g % RING, hh, :].rearrange("p (i m) -> p i m", m=M),
                                                ps[0:r, 4 + hh, :].rearrange("p (i m) -> p i m", m=M),
                                                nrm.to_broadcast([r, HPH, M]), ALU.subtract).then_inc(karg_ready, 1)

                for c in range(CHUNKS):
                    exponents(c, 0)
                    queries(b, c, 1)
                    if c + 1 < CHUNKS:
                        split_x(b, c + 1)
                    exponents(c, 1)
                    if c == CHUNKS - 1:
                        squares(b, c, 1)
                    exponents(c, 2)
                    if c + 1 < CHUNKS:
                        squares(b, c, 1)
                        keys(b, c + 1, 0)
                        keys(b, c + 1, 1)
                        queries(b, c + 1, 0)
                        norms(b, c + 1)
                        squares(b, c + 1, 0)
                dve.wait_ge(kvall_done, b + 1)
                for hh in range(KD):
                    nc.vector.tensor_tensor(kvm[:, hh, :], ps[:, 6 + hh, 0:P], mask, ALU.mult)
                    ins = nc.vector.scalar_tensor_tensor(out=kvm[:, KD + hh, :], in0=ps[:, 6 + hh, P:2 * P],
                                                         scalar=KERNEL_EPS * L, in1=mask, op0=ALU.add, op1=ALU.mult)
                ins.then_inc(kvm_ready, 1)
                dve.wait_ge(kvm_ready, b + 1)
                then(nc.vector.tensor_reduce(kvr[:, 0, :], kvm[:], AX.X, ALU.add))
                nc.vector.tensor_scalar(kvr[:, 1, :], kvr[:, 0, :], KERNEL_EPS, None, ALU.mult)
                dve.wait_ge(kvT_turned, b + 1)
                nc.vector.tensor_copy(kvs[:].rearrange("p a m -> p (a m)"), ps[:, 2, :]).then_inc(kvs_ready, 1)
                dve.wait_ge(kvs_ready, b + 1)

                def attend(c):
                    halves_done = [0, 0]

                    def of(hh):
                        dve.wait_ge(dve_step, base[0] + halves_done[hh])

                    def done(hh, ins):
                        ins.then_inc(dve_step, 1)
                        steps[0] += 1
                        halves_done[hh] = steps[0]

                    dens = [den[c][:, hh * N:(hh + 1) * N] for hh in range(KD)]
                    for hh in range(KD):
                        dve.wait_ge(den_ready, (b * CHUNKS + c) * KD + hh + 1)
                        if c >= 1 and hh == 0:
                            dve.wait_ge(att_ready, b * CHUNKS + c)
                        done(hh, nc.vector.transpose(rden[:, hh, :], dens[hh]))
                    for hh in range(KD):
                        of(hh)
                        done(hh, nc.vector.reciprocal(rec[:, hh * NB // KD:(hh + 1) * NB // KD, :],
                                                      rden[:, hh, :].rearrange("p (n i d) -> p n i d", i=2, d=DK)[:, :, :, 0]))
                    for hh in range(KD):
                        of(hh)
                        done(hh, nc.vector.tensor_copy(dens[hh].rearrange("p (n d) -> p n d", d=DK),
                                                       rec[:, hh * NB // KD:(hh + 1) * NB // KD, :].rearrange("p n (i o) -> p (n i) o", o=1)
                                                       .to_broadcast([P, 2 * NB // KD, DK])))
                    for hh in range(KD):
                        of(hh)
                        ins = nc.vector.transpose(rden[:, hh, :], dens[hh])
                        if c != 1:
                            done(hh, ins)
                    if c == 1:
                        ins.then_inc(rden_ready, 1)
                        return
                    for hh in range(KD):
                        of(hh)
                        dve.wait_ge(nd_ready, (b * CHUNKS + c) * KD + hh + 1)
                        ins = nc.vector.tensor_tensor(att[:, c, hh, :], att[:, c, hh, :], rden[:, hh, :], ALU.mult)
                    ins.then_inc(att_ready, 1)

                def residual(c):
                    g, r = c * TILES, ROWS[2]
                    dve.wait_ge(wo_done, b * G + g + 2)
                    if g == 0:
                        dve.wait_ge(out_stored, b * 16 * 2 * CHUNKS + 1)
                    nc.vector.tensor_tensor(h2[:, g:g + 2, :], two_tiles(WO_BANKS[c]), hb[:, bass.ds(b * G + g, 2), :], ALU.add).then_inc(h2_ready, 2)
                    dve.wait_ge(wo_done, b * G + g + 3)
                    hb_g = hb[0:r, bass.ds(b * G + g + 2, 1), :].rearrange("p o d -> p (o d)")
                    nc.vector.tensor_tensor(h2[0:r, g + 2, :], ps[0:r, WO_BANKS[c] + 1, 0:D], hb_g, ALU.add).then_inc(h2_ready, 1)
                    dve.wait_ge(h2_ready, b * G + (c + 1) * TILES)
                    statistics(h2, c).then_inc(var2_ready, 1)

                def normalise_h2(c):
                    dve.wait_ge(rstd2_ready, b * CHUNKS + c + 1)
                    if c >= 2:
                        dve.wait_ge(xln2T_turned, b * CHUNKS + c - 1)
                    normalise(h2, c, c % 2).then_inc(xln2_ready, 1)

                def low_rank(c):
                    dve.wait_ge(phi_ready, b * CHUNKS + c + 1)
                    up = slice(RANK, P)
                    nc.vector.tensor_tensor(pS[up, c % 2, :], ps[up, 2, 0:N], pS[up, c % 2, :].bitcast(F32),
                                            ALU.subtract).then_inc(p_ready, 1)

                def low_result(c):
                    dve.wait_ge(u_done, b * CHUNKS + c + 1)
                    nc.vector.tensor_copy(uT[:], ps[:, 1, 0:N]).then_inc(u_ready, 1)

                def result(c):
                    dve.wait_ge(h2b_ready, b * G + (c + 1) * TILES)
                    g, r = c * TILES, ROWS[2]
                    dve.wait_ge(y_done, b * G + g + 2)
                    nc.vector.tensor_tensor(h2[:, g:g + 2, :], two_tiles(0), h2[:, g:g + 2, :], ALU.add).then_inc(fin_ready, 2)
                    dve.wait_ge(y_done, b * G + g + 3)
                    nc.vector.tensor_tensor(h2[0:r, g + 2, :], ps[0:r, 1, 0:D], h2[0:r, g + 2, :], ALU.add).then_inc(fin_ready, 1)

                attend(0)
                attend(1)
                residual(0)
                attend(2)
                residual(1)
                low_rank(0)
                normalise_h2(1)
                residual(2)
                normalise_h2(2)
                low_rank(1)
                low_result(0)
                result(0)
                low_rank(2)
                low_result(1)
                result(1)
                if more:
                    split_x(b, CHUNKS)
                    keys(b, CHUNKS, 0)
                    keys(b, CHUNKS, 1)
                low_result(2)
                result(2)
                if more:
                    queries(b, CHUNKS, 0)
                    norms(b, CHUNKS)
                    squares(b, CHUNKS, 0)
                    assert steps[0] == DVE_STEPS, steps[0]

            with dve.Fori(0, B - 1) as b:
                batch_entry(b, True)
            batch_entry(B - 1, False)

        @block.tensor
        def _(pe):
            def mm3(dst, a, b, cols_a, cols_b, start=True, stop=True):
                nc.tensor.matmul(dst, a(1, cols_a), b(0, cols_b), start=start, stop=False)
                nc.tensor.matmul(dst, a(0, cols_a), b(1, cols_b), start=False, stop=False)
                return nc.tensor.matmul(dst, a(0, cols_a), b(0, cols_b), start=False, stop=stop)

            def row_tile(t, bank):
                return ps[0:ROWS[t], bank + t // 2, t % 2 * D:(t % 2 + 1) * D]

            pe.wait_ge(tok_in, 16)
            pe.wait_ge(consts_set, 1)

            def turn_x(c):
                cc = c % CHUNKS
                pe.wait_ge(x_in[c], 32)
                if cc == CHUNKS - 1:
                    pe.wait_ge(txt_in[c // CHUNKS], 16)
                if c >= 1:
                    pe.wait_ge(xT_ready, c)
                for k in range(KD):
                    for t in range(TILES):
                        g, r = cc * TILES + t, ROWS[t]
                        ins = nc.tensor.transpose(ps[:, k, tile_cols(t)], xh[c // CHUNKS][0:r, g, k * P:(k + 1) * P], idn[0:r, 0:r])
                ins.then_inc(xT_turned, 1)

            def turn_xln(c):
                pe.wait_ge(xln_ready, c + 1)
                if c >= 1:
                    pe.wait_ge(xlnT_ready, c)
                for k in range(KD):
                    for t in range(TILES):
                        r = ROWS[t]
                        ins = nc.tensor.transpose(ps[:, 6 + k, tile_cols(t)], xln[0:r, c % 2, t, k * P:(k + 1) * P], idn[0:r, 0:r])
                ins.then_inc(xlnT_turned, 1)

            def values(c):
                pe.wait_ge(xlnT_ready, c + 1)
                if c == 0:
                    pe.wait_ge(row_in, 16)
                    pe.wait_ge(pads_set, B)
                if c >= 1:
                    pe.wait_ge(v_ready, c * TILES)
                for t in range(TILES):
                    r = ROWS[t]
                    for k in range(KD):
                        ins = nc.tensor.matmul(row_tile(t, 4), xlnT[:, c, k, tile_cols(t)], wv[:, k, :],
                                               start=k == 0, stop=k == KD - 1)
                    ins.then_inc(v_done, 1)

            turn_x(0)
            for c in range(NC):
                pe.wait_ge(xT_ready, c + 1)
                if c >= 1:
                    pe.wait_ge(tanh_done, c)
                for k in range(KD):
                    ins = nc.tensor.matmul(ps[:, 2, 0:N], w1[:, k, :], xT[:, c % 2, k, :], start=k == 0, stop=k == KD - 1)
                ins.then_inc(tok_done, 1)
                if c + 1 < NC:
                    turn_x(c + 1)
                if c == 2:
                    turn_xln(0)
                pe.wait_ge(tanh_done, c + 1)
                if c >= 1:
                    pe.wait_ge(logit_ready, c)
                for t in range(TILES):
                    g = c % CHUNKS * TILES + t
                    ins = nc.tensor.matmul(ps[:, 3, g:g + 1], hT[:, c % 2, t * P:(t + 1) * P], w2, start=True, stop=True)
                ins.then_inc(energy_done, 1)
                if c >= 2:
                    values(c - 2)
                if c >= 2:
                    turn_xln(c - 1)
            def keys(b, c, hh):
                pe.wait_ge(xs_ready, b * CHUNKS + c + 1)
                if c >= 1:
                    pe.wait_ge(q_ready, (b * CHUNKS + c - 1) * KD + hh + 1)
                for k in range(KD):
                    ins = mm3(ps[:, 2 + hh, 0:N], lambda i, s: wk[:, i, k, s], lambda i, s: xs[:, i, k, s],
                              slice(hh * P, (hh + 1) * P), slice(0, N), k == 0, k == KD - 1)
                ins.then_inc(k_done, 1)

            def queries(b, c, hh):
                pe.wait_ge(k_ready, (b * CHUNKS + c) * KD + hh + 1)
                for k in range(KD):
                    ins = mm3(ps[:, 2 + hh, 0:N], lambda i, s: wq[:, i, k, s], lambda i, s: xs[:, i, k, s],
                              slice(hh * P, (hh + 1) * P), slice(0, N), k == 0, k == KD - 1)
                ins.then_inc(q_done, 1)

            def norms(b, c, bank=KN_BANKS[1]):
                pe.wait_ge(ksq_ready, (b * CHUNKS + c + 1) * KD)
                if c >= 1:
                    pe.wait_ge(karg_ready, (b * CHUNKS + c) * TILES * KD - 1)
                for hh in range(KD):
                    ins = nc.tensor.matmul(ps[hh * BLK:(hh + 1) * BLK, bank, 0:N], ncol, ksq[:, hh, :], start=True, stop=True,
                                           tile_position=(0, hh * BLK))
                ins.then_inc(kn_done, 1)

            def turn_norms(b, c, bank=KN_BANKS[1]):
                pe.wait_ge(knT_ready, b * CHUNKS + c + 1)
                if c >= 1:
                    pe.wait_ge(karg_ready, (b * CHUNKS + c) * TILES * KD)
                for t in range(TILES):
                    ins = nc.tensor.transpose(ps[0:ROWS[t], bank + 1, t * P:(t + 1) * P], knT[:, tile_cols(t)], idn)
                ins.then_inc(kn_turned, 1)

            pe.wait_ge(hi_split, 4)
            pe.wait_ge(lo_split, 4)
            pe.wait_ge(logit_ready, NC)
            keys(0, 0, 0)
            keys(0, 0, 1)
            values(NC - 2)
            pe.wait_ge(xT_ready, NC)
            pe.wait_ge(rest_in, 16)
            norms(0, 0, KN_BANKS[0])
            turn_xln(NC - 1)
            queries(0, 0, 0)
            turn_norms(0, 0, KN_BANKS[0])
            values(NC - 1)
            queries(0, 0, 1)
            pe.wait_ge(kn_ready, 1)
            pe.wait_ge(v_ready, NC * TILES)

            def batch_entry(b, more):
                def kproj(c, t):
                    g, r = c * TILES + t, ROWS[t]
                    if t == 0:
                        pe.wait_ge(k_ready, (b * CHUNKS + c + 1) * KD)
                    for hh in range(KD):
                        if t == 0:
                            pe.wait_ge(kn_ready, b * CHUNKS + c + 1)
                        else:
                            pe.wait_ge(karg_ready, (b * G + g - 1) * KD + hh + 1)
                        for u in range(2):
                            dst = ps[0:r, 4 + hh, 2 * P * u:2 * P * (u + 1)]
                            nc.tensor.matmul(dst, ks[:, u, hh, tile_cols(t)], quad[:, 1], start=True, stop=False)
                            ins = nc.tensor.matmul(dst, ks[:, u, hh, tile_cols(t)], quad[:, 0], start=False, stop=True)
                        ins.then_inc(kproj_done, 1)

                def qproj(c, p):
                    hh, j = divmod(p, PPH)
                    if p == 0:
                        pe.wait_ge(fin_ready, b * G + 1)
                    if c > 0 or p >= 2:
                        pe.wait_ge(qphi_ready, (b * CHUNKS + c) * PAIRS + p - 1)
                    pe.wait_ge(q_ready, (b * CHUNKS + c) * KD + hh + 1)
                    u, v = divmod(j, 2)
                    s = slice(v * P, (v + 1) * P)
                    nc.tensor.matmul(ps[:, p % 2, 0:N], quad[:, 1, s], qs[:, u, hh, :], start=True, stop=False)
                    nc.tensor.matmul(ps[:, p % 2, 0:N], quad[:, 0, s], qs[:, u, hh, :], start=False, stop=False)
                    pe.wait_ge(qsq_ready, (b * CHUNKS + c) * KD + hh + 1)
                    nc.tensor.matmul(ps[:, p % 2, 0:N], quad[:, 2, s], qsq[:, u, hh, :], start=False, stop=True).then_inc(qproj_done, 1)

                def kv(c, t):
                    g, r = c * TILES + t, ROWS[t]
                    pe.wait_ge(kphi_ready, (b * G + g + 1) * KD)
                    for p in range(PAIRS):
                        hh, j = divmod(p, PPH)
                        ins = nc.tensor.matmul(ps[BLK * j:BLK * (j + 1), 6 + hh, 0:P], vs[0][0:r, g, BLK * p:BLK * (p + 1)],
                                               kphi[0:r, g % RING, hh, j * P:(j + 1) * P], start=g == 0, stop=False,
                                               tile_position=(0, BLK * j), skip_group_check=True)
                    ins.then_inc(kv_done, 1)

                def kv_sums():
                    pe.wait_ge(ksum_ready, (b + 1) * (G - 1))
                    for p in range(PAIRS):
                        hh, j = divmod(p, PPH)
                        nc.tensor.matmul(ps[BLK * j:BLK * (j + 1), 6 + hh, 0:P], vs[0][:, G, BLK * p:BLK * (p + 1)], epsm[:],
                                         start=False, stop=True, tile_position=(0, BLK * j), skip_group_check=True)
                    for p in range(PAIRS):
                        hh, j = divmod(p, PPH)
                        nc.tensor.matmul(ps[BLK * j:BLK * (j + 1), 6 + hh, P:2 * P], ones[:], ksum[:, p * P:(p + 1) * P],
                                         start=False, stop=False, tile_position=(0, BLK * j), skip_group_check=True)
                    r, slot = ROWS[TILES - 1], (G - 1) % RING
                    for p in range(PAIRS):
                        hh, j = divmod(p, PPH)
                        ins = nc.tensor.matmul(ps[BLK * j:BLK * (j + 1), 6 + hh, P:2 * P], ones[0:r, :],
                                               kphi[0:r, slot, hh, j * P:(j + 1) * P],
                                               start=False, stop=True, tile_position=(0, BLK * j), skip_group_check=True)
                    ins.then_inc(kvall_done, 1)

                def kv_turn():
                    pe.wait_ge(kvm_ready, b + 1)
                    pe.wait_ge(q_ready, (b + 1) * CHUNKS * KD)
                    for i in range(2 * KD):
                        ins = nc.tensor.transpose(ps[:, 2, i * P:(i + 1) * P], kvm[:, i, :], idn)
                    ins.then_inc(kvT_turned, 1)

                def numden(c, hh):
                    if c == 0 and hh == 0:
                        pe.wait_ge(kvs_ready, b + 1)
                    if c == CHUNKS - 1:
                        pe.wait_ge(qphi_ready, (b + 1) * CHUNKS * PAIRS)
                    if 2 * c + hh >= 3:
                        pe.wait_ge(nd_ready, b * CHUNKS * KD + 2 * c + hh - 2)
                    for s in range(2):
                        for j in range(PPH):
                            ins = nc.tensor.matmul(ps[BLK * j:BLK * (j + 1), ND_BANKS[c][hh] + s, 0:N],
                                                   kvs[:, s * KD + hh, BLK * j:BLK * (j + 1)],
                                                   work[:, c, hh * PPH + j, :], start=True, stop=True,
                                                   tile_position=(0, BLK * j))
                    ins.then_inc(nd_done, 1)

                def project(c, tiles=range(TILES)):
                    pe.wait_ge(att_ready, b * CHUNKS + c + 1)
                    if c == 0:
                        pe.wait_ge(qphi_ready, (b + 1) * CHUNKS * PAIRS)
                    elif c == 1:
                        pe.wait_ge(nd_ready, (b + 1) * CHUNKS * KD - 1)
                    else:
                        pe.wait_ge(h2_ready, b * G + TILES)
                    for t in tiles:
                        for k in range(KD):
                            ins = nc.tensor.matmul(row_tile(t, WO_BANKS[c]), att[:, c, k, tile_cols(t)], wo[:, k, :],
                                                   start=k == 0, stop=k == KD - 1)
                        ins.then_inc(wo_done, 1)

                def turn_xln2(c):
                    pe.wait_ge(xln2_ready, b * CHUNKS + c + 1)
                    if c == 0:
                        pe.wait_ge(nd_ready, b * CHUNKS * KD + 4)
                    else:
                        pe.wait_ge(p_ready, b * CHUNKS + c)
                    for k in range(KD):
                        for t in range(TILES):
                            r = ROWS[t]
                            ins = nc.tensor.transpose(ps[:, 2 + k, tile_cols(t)], xln[0:r, c % 2, t, k * P:(k + 1) * P], idn[0:r, 0:r])
                    ins.then_inc(xln2T_turned, 1)

                def down_in(c):
                    pe.wait_ge(xln2T_ready, b * CHUNKS + c + 1)
                    for k in range(KD):
                        ins = nc.tensor.matmul(ps[:, 2, 0:N], u1[:, k, :], xln2T[:, k, :], start=k == 0, stop=k == KD - 1)
                    ins.then_inc(p_done, 1)

                def up(c, i):
                    if i == 0:
                        pe.wait_ge(p_ready, b * CHUNKS + c + 1)
                    if c == 0 and i < 4:
                        pe.wait_ge(h2_ready, b * G + 2 * TILES)
                    else:
                        pe.wait_ge(gelu_ready, (b * CHUNKS + c) * FT + i - 3)
                    f = FORDER[i]
                    nc.tensor.matmul(ps[:, 4 + i % 4, 0:N], v1[:, 1, f * P:(f + 1) * P], pS[:, c % 2, :], start=True, stop=False)
                    nc.tensor.matmul(ps[:, 4 + i % 4, 0:N], v1[:, 0, f * P:(f + 1) * P], pS[:, c % 2, :], start=False,
                                     stop=True).then_inc(ff_done, 1)

                def down(c, i):
                    if i == 0:
                        if c == 0:
                            pe.wait_ge(h2_ready, (b + 1) * G)
                        else:
                            pe.wait_ge(fin_ready, b * G + c * TILES + 1)
                    pe.wait_ge(gelu_ready, (b * CHUNKS + c) * FT + i + 1)
                    side = i % 2
                    ins = nc.tensor.matmul(ps[RANK * side:RANK * (side + 1), 1, 0:N], u2[:, FORDER[i], :], work[:, c, i, :],
                                           start=i < 2, stop=i >= FT - 2, tile_position=(0, RANK * side))
                    if i == FT - 1:
                        ins.then_inc(u_done, 1)

                def up_out(c):
                    pe.wait_ge(u_ready, b * CHUNKS + c + 1)
                    for t in range(TILES):
                        nc.tensor.matmul(row_tile(t, 0), uT[:, tile_cols(t)], v2, start=True, stop=True).then_inc(y_done, 1)

                for c in range(CHUNKS - 1):
                    kproj(c, 0)
                    qproj(c, 0)
                    qproj(c, 1)
                    kproj(c, 1)
                    qproj(c, 2)
                    kv(c, 0)
                    qproj(c, 3)
                    kproj(c, 2)
                    keys(b, c + 1, 0)
                    kv(c, 1)
                    keys(b, c + 1, 1)
                    kv(c, 2)
                    qproj(c, 4)
                    qproj(c, 5)
                    queries(b, c + 1, 0)
                    norms(b, c + 1)
                    qproj(c, 6)
                    queries(b, c + 1, 1)
                    turn_norms(b, c + 1)
                    qproj(c, 7)
                c = CHUNKS - 1
                kproj(c, 0)
                qproj(c, 0)
                qproj(c, 1)
                kproj(c, 1)
                qproj(c, 2)
                kv(c, 0)
                qproj(c, 3)
                kproj(c, 2)
                kv(c, 1)
                qproj(c, 4)
                qproj(c, 5)
                kv(c, 2)
                kv_sums()
                qproj(c, 6)
                kv_turn()
                qproj(c, 7)
                numden(0, 0)
                numden(0, 1)
                numden(1, 0)
                numden(1, 1)
                numden(2, 0)
                project(0)
                numden(2, 1)
                project(1)
                turn_xln2(0)
                project(2, [0])
                down_in(0)
                project(2, [1, 2])
                for c in range(CHUNKS):
                    for i in range(0 if c == 0 else 2, 4):
                        up(c, i)
                    if c + 1 < CHUNKS:
                        turn_xln2(c + 1)
                    down(c, 0)
                    down(c, 1)
                    up(c, 4)
                    up(c, 5)
                    if c + 1 < CHUNKS:
                        down_in(c + 1)
                    down(c, 2)
                    down(c, 3)
                    up(c, 6)
                    up(c, 7)
                    if c + 1 < CHUNKS:
                        for i in range(4, FT):
                            down(c, i)
                        up(c + 1, 0)
                        up(c + 1, 1)
                        up_out(c)
                if more:
                    keys(b, CHUNKS, 0)
                    keys(b, CHUNKS, 1)
                for i in range(4, FT):
                    down(CHUNKS - 1, i)
                if more:
                    norms(b, CHUNKS)
                    queries(b, CHUNKS, 0)
                up_out(CHUNKS - 1)
                if more:
                    turn_norms(b, CHUNKS)
                    queries(b, CHUNKS, 1)
                    pe.wait_ge(v_moved, 16 * (b + 1))

            with pe.Fori(0, B - 1) as b:
                batch_entry(b, True)
            batch_entry(B - 1, False)


_OUT = ((2, 1056, 256), "float32")


def kernel(**inputs):
    import numpy as np
    import concourse.bacc as bacc
    from concourse.bass_utils import run_bass_kernel_spmd

    arg = {k.replace("L0_", ""): np.asarray(v) for k, v in inputs.items()}
    DK, M = 16, 64

    def tall(a):
        return a.reshape(-1, 128, a.shape[1]).transpose(1, 0, 2).reshape(128, -1)

    def same_rows(a):
        return np.broadcast_to(a[None, :], (128, a.shape[0]))

    def columns(a):
        return a.reshape(-1, 128).T

    orf = np.zeros((128, 8 * M), np.float32)
    for i in range(8):
        orf[DK * i:DK * (i + 1), M * i:M * (i + 1)] = arg["attn_orf"].T
    own = np.kron(np.eye(128 // DK), np.ones((DK, M)))
    cols = np.zeros((128, 32))
    cols[:, :8] = np.kron(np.eye(128 // DK), np.ones((DK, 1)))
    pair = np.kron(np.eye(2), np.ones((DK, M)))
    packed = {
        "ident": np.eye(128, dtype=np.float32),
        "W1": tall(arg["tok_W1"]), "b1": columns(arg["tok_b1"]), "W2": arg["tok_W2"],
        "b2": np.broadcast_to(arg["tok_b2"][None, :], (128, 1)),
        "WkT": tall(arg["attn_Wk"].T), "WqT": tall(arg["attn_Wq"].T), "WvT": tall(arg["attn_Wv"].T), "WoT": tall(arg["attn_Wo"].T),
        "bk": columns(arg["attn_bk"]), "bq": columns(arg["attn_bq"]), "bv": same_rows(arg["attn_bv"]), "bo": same_rows(arg["attn_bo"]),
        "orf_quad": np.concatenate([orf[:64, :256]] * 2),
        "norm_quad": np.concatenate([own[:64, :256] * (-0.5 / DK ** 0.5)] * 2).astype(np.float32),
        "norm_cols": (cols * (0.5 / DK ** 0.5)).astype(np.float32),
        "head_mask": (np.tile(pair, (4, 1)) / M).astype(np.float32),
        "U1": tall(np.concatenate([arg["ffn_U1"], arg["ffn_U1"]], axis=1)),
        "V1": np.concatenate([arg["ffn_V1"], arg["ffn_V1"]], axis=0), "b1f": columns(arg["ffn_b1"]),
        "U2": tall(arg["ffn_U2"]), "V2": np.concatenate([arg["ffn_V2"], arg["ffn_V2"]], axis=0), "b2f": same_rows(arg["ffn_b2"]),
    }

    def pack(columns_of):
        return np.concatenate([packed[n] for n, _ in columns_of], axis=1)

    host = {"x": arg["x"], "ids": arg["x_txt"].T, "emb": arg["txt_w"], "tok_w": pack(TOK_COLS), "raw_w": pack(RAW_COLS),
            "row_w": pack(ROW_COLS), "rest_w": pack(REST_COLS)}
    nc = bacc.Bacc("TRN2", target_bir_lowering=False, num_devices=1)
    arrays, args = {}, []
    for name, a in host.items():
        a = np.ascontiguousarray(a)
        arrays[f"in_{name}"] = a
        args.append(nc.dram_tensor(f"in_{name}", a.shape, mybir.dt.from_np(a.dtype), kind="ExternalInput").ap())
    args.append(nc.dram_tensor("out_0", _OUT[0], mybir.dt.float32, kind="ExternalOutput").ap())
    build(nc, *args)
    r = run_bass_kernel_spmd(nc, [arrays], core_ids=[0])
    return r.results[0]["out_0"]
```
